# Optimizing a Trainium2 kernel written in Bass

```python
import numpy as np
import jax
import jax.numpy as jnp

def _softmax(x, axis=-1):
    return jax.nn.softmax(x, axis=axis)

def _gelu(x):
    return jax.nn.gelu(x, approximate=True)

def _silu(x):
    return jax.nn.silu(x)

def _sigmoid(x):
    return jax.nn.sigmoid(x)

def _layernorm(x, axis=-1, eps=1e-05):
    m = jnp.mean(x, axis=axis, keepdims=True)
    v = jnp.var(x, axis=axis, keepdims=True)
    return (x - m) / jnp.sqrt(v + eps)

def _scatter_add(tgt, idx, src, axis=0):
    return tgt.at[idx].add(src)

def _segment_sum(src, seg, n):
    return jax.ops.segment_sum(src, seg, n)
kernel_name = 'mk_dlrm_tower_d1_rec_r8_556bc9'

def setup_inputs(seed: int=0):
    np.random.seed(seed)
    _w = jnp.asarray

    def _rec_inputs():
        import jax
        import jax.numpy as jnp
        _tk = jax.random.key(seed)
        dense_ctx = jax.random.normal(jax.random.fold_in(_tk, 190), (2048, 16), jnp.float32)
        ids = jnp.stack([jax.random.randint(jax.random.fold_in(_tk, 200 + f), (2048,), 0, v, jnp.int32) for f, v in enumerate([12500, 12500, 125000, 1250, 125000, 1000, 12500, 12500, 125000, 1000, 1250, 1250, 125000, 125000, 12500, 12500, 1250, 1000, 1250, 12500, 12500, 1000, 125000, 1250, 125000, 1000, 1250, 1000, 1250, 1000, 12500, 125000, 1250, 1000, 12500, 1000, 1000, 1250, 1250])], axis=1)
        tbl_0 = 0.05 * jax.random.normal(jax.random.fold_in(_tk, 500 + 0), (12500, 16), jnp.float32)
        tbl_1 = 0.05 * jax.random.normal(jax.random.fold_in(_tk, 500 + 1), (12500, 16), jnp.float32)
        tbl_2 = 0.05 * jax.random.normal(jax.random.fold_in(_tk, 500 + 2), (125000, 16), jnp.float32)
        tbl_3 = 0.05 * jax.random.normal(jax.random.fold_in(_tk, 500 + 3), (1250, 16), jnp.float32)
        tbl_4 = 0.05 * jax.random.normal(jax.random.fold_in(_tk, 500 + 4), (125000, 16), jnp.float32)
        tbl_5 = 0.05 * jax.random.normal(jax.random.fold_in(_tk, 500 + 5), (1000, 16), jnp.float32)
        tbl_6 = 0.05 * jax.random.normal(jax.random.fold_in(_tk, 500 + 6), (12500, 16), jnp.float32)
        tbl_7 = 0.05 * jax.random.normal(jax.random.fold_in(_tk, 500 + 7), (12500, 16), jnp.float32)
        tbl_8 = 0.05 * jax.random.normal(jax.random.fold_in(_tk, 500 + 8), (125000, 16), jnp.float32)
        tbl_9 = 0.05 * jax.random.normal(jax.random.fold_in(_tk, 500 + 9), (1000, 16), jnp.float32)
        tbl_10 = 0.05 * jax.random.normal(jax.random.fold_in(_tk, 500 + 10), (1250, 16), jnp.float32)
        tbl_11 = 0.05 * jax.random.normal(jax.random.fold_in(_tk, 500 + 11), (1250, 16), jnp.float32)
        tbl_12 = 0.05 * jax.random.normal(jax.random.fold_in(_tk, 500 + 12), (125000, 16), jnp.float32)
        tbl_13 = 0.05 * jax.random.normal(jax.random.fold_in(_tk, 500 + 13), (125000, 16), jnp.float32)
        tbl_14 = 0.05 * jax.random.normal(jax.random.fold_in(_tk, 500 + 14), (12500, 16), jnp.float32)
        tbl_15 = 0.05 * jax.random.normal(jax.random.fold_in(_tk, 500 + 15), (12500, 16), jnp.float32)
        tbl_16 = 0.05 * jax.random.normal(jax.random.fold_in(_tk, 500 + 16), (1250, 16), jnp.float32)
        tbl_17 = 0.05 * jax.random.normal(jax.random.fold_in(_tk, 500 + 17), (1000, 16), jnp.float32)
        tbl_18 = 0.05 * jax.random.normal(jax.random.fold_in(_tk, 500 + 18), (1250, 16), jnp.float32)
        tbl_19 = 0.05 * jax.random.normal(jax.random.fold_in(_tk, 500 + 19), (12500, 16), jnp.float32)
        tbl_20 = 0.05 * jax.random.normal(jax.random.fold_in(_tk, 500 + 20), (12500, 16), jnp.float32)
        tbl_21 = 0.05 * jax.random.normal(jax.random.fold_in(_tk, 500 + 21), (1000, 16), jnp.float32)
        tbl_22 = 0.05 * jax.random.normal(jax.random.fold_in(_tk, 500 + 22), (125000, 16), jnp.float32)
        tbl_23 = 0.05 * jax.random.normal(jax.random.fold_in(_tk, 500 + 23), (1250, 16), jnp.float32)
        tbl_24 = 0.05 * jax.random.normal(jax.random.fold_in(_tk, 500 + 24), (125000, 16), jnp.float32)
        tbl_25 = 0.05 * jax.random.normal(jax.random.fold_in(_tk, 500 + 25), (1000, 16), jnp.float32)
        tbl_26 = 0.05 * jax.random.normal(jax.random.fold_in(_tk, 500 + 26), (1250, 16), jnp.float32)
        tbl_27 = 0.05 * jax.random.normal(jax.random.fold_in(_tk, 500 + 27), (1000, 16), jnp.float32)
        tbl_28 = 0.05 * jax.random.normal(jax.random.fold_in(_tk, 500 + 28), (1250, 16), jnp.float32)
        tbl_29 = 0.05 * jax.random.normal(jax.random.fold_in(_tk, 500 + 29), (1000, 16), jnp.float32)
        tbl_30 = 0.05 * jax.random.normal(jax.random.fold_in(_tk, 500 + 30), (12500, 16), jnp.float32)
        tbl_31 = 0.05 * jax.random.normal(jax.random.fold_in(_tk, 500 + 31), (125000, 16), jnp.float32)
        tbl_32 = 0.05 * jax.random.normal(jax.random.fold_in(_tk, 500 + 32), (1250, 16), jnp.float32)
        tbl_33 = 0.05 * jax.random.normal(jax.random.fold_in(_tk, 500 + 33), (1000, 16), jnp.float32)
        tbl_34 = 0.05 * jax.random.normal(jax.random.fold_in(_tk, 500 + 34), (12500, 16), jnp.float32)
        tbl_35 = 0.05 * jax.random.normal(jax.random.fold_in(_tk, 500 + 35), (1000, 16), jnp.float32)
        tbl_36 = 0.05 * jax.random.normal(jax.random.fold_in(_tk, 500 + 36), (1000, 16), jnp.float32)
        tbl_37 = 0.05 * jax.random.normal(jax.random.fold_in(_tk, 500 + 37), (1250, 16), jnp.float32)
        tbl_38 = 0.05 * jax.random.normal(jax.random.fold_in(_tk, 500 + 38), (1250, 16), jnp.float32)
        _rk = jax.random.fold_in(_tk, 7)
        W_top1 = 0.0606339 * jax.random.normal(jax.random.fold_in(_tk, 801), (272, 512), jnp.float32)
        W_top2 = 0.0441942 * jax.random.normal(jax.random.fold_in(_tk, 802), (512, 256), jnp.float32)
        W_top3 = 0.0625 * jax.random.normal(jax.random.fold_in(_tk, 803), (256, 1), jnp.float32)
        b_top1 = jnp.zeros((512,), jnp.float32)
        b_top2 = jnp.zeros((256,), jnp.float32)
        return (dense_ctx, ids, tbl_0, tbl_1, tbl_2, tbl_3, tbl_4, tbl_5, tbl_6, tbl_7, tbl_8, tbl_9, tbl_10, tbl_11, tbl_12, tbl_13, tbl_14, tbl_15, tbl_16, tbl_17, tbl_18, tbl_19, tbl_20, tbl_21, tbl_22, tbl_23, tbl_24, tbl_25, tbl_26, tbl_27, tbl_28, tbl_29, tbl_30, tbl_31, tbl_32, tbl_33, tbl_34, tbl_35, tbl_36, tbl_37, tbl_38, W_top1, b_top1, W_top2, b_top2, W_top3)
    dense_ctx, ids, tbl_0, tbl_1, tbl_2, tbl_3, tbl_4, tbl_5, tbl_6, tbl_7, tbl_8, tbl_9, tbl_10, tbl_11, tbl_12, tbl_13, tbl_14, tbl_15, tbl_16, tbl_17, tbl_18, tbl_19, tbl_20, tbl_21, tbl_22, tbl_23, tbl_24, tbl_25, tbl_26, tbl_27, tbl_28, tbl_29, tbl_30, tbl_31, tbl_32, tbl_33, tbl_34, tbl_35, tbl_36, tbl_37, tbl_38, W_top1, b_top1, W_top2, b_top2, W_top3 = _rec_inputs()

    def _L0_rec_setup():
        import jax, jax.numpy as jnp
        import numpy as np
        B, F0, D = (256, 39, 16)
        LAYER_SIZES = [128, 128, 128]
        key = jax.random.key(seed)
        ks = jax.random.split(key, 1 + 2 * len(LAYER_SIZES))
        inputs = jax.random.normal(ks[0], (B, F0, D), dtype=jnp.float32)
        out = {'inputs': inputs}
        field_nums = [F0]
        for i, size in enumerate(LAYER_SIZES):
            fk = field_nums[-1]
            fan_in = F0 * fk
            scale = np.sqrt(2.0 / (fan_in + size)).astype(np.float32)
            out[f'w{i}'] = jax.random.normal(ks[1 + 2 * i], (F0, fk, size), dtype=jnp.float32) * scale
            out[f'b{i}'] = jnp.zeros((size,), dtype=jnp.float32)
            field_nums.append(size // 2)
        return out
    _L0_rec_all = _L0_rec_setup()
    _L0_rec_in = {k: v for k, v in _L0_rec_all.items() if k in ('w0', 'w1', 'w2', 'b0', 'b1', 'b2')}
    del _L0_rec_all
    return {'dense_ctx': dense_ctx, 'ids': ids, 'tbl_0': tbl_0, 'tbl_1': tbl_1, 'tbl_2': tbl_2, 'tbl_3': tbl_3, 'tbl_4': tbl_4, 'tbl_5': tbl_5, 'tbl_6': tbl_6, 'tbl_7': tbl_7, 'tbl_8': tbl_8, 'tbl_9': tbl_9, 'tbl_10': tbl_10, 'tbl_11': tbl_11, 'tbl_12': tbl_12, 'tbl_13': tbl_13, 'tbl_14': tbl_14, 'tbl_15': tbl_15, 'tbl_16': tbl_16, 'tbl_17': tbl_17, 'tbl_18': tbl_18, 'tbl_19': tbl_19, 'tbl_20': tbl_20, 'tbl_21': tbl_21, 'tbl_22': tbl_22, 'tbl_23': tbl_23, 'tbl_24': tbl_24, 'tbl_25': tbl_25, 'tbl_26': tbl_26, 'tbl_27': tbl_27, 'tbl_28': tbl_28, 'tbl_29': tbl_29, 'tbl_30': tbl_30, 'tbl_31': tbl_31, 'tbl_32': tbl_32, 'tbl_33': tbl_33, 'tbl_34': tbl_34, 'tbl_35': tbl_35, 'tbl_36': tbl_36, 'tbl_37': tbl_37, 'tbl_38': tbl_38, 'W_top1': W_top1, 'b_top1': b_top1, 'W_top2': W_top2, 'b_top2': b_top2, 'W_top3': W_top3, 'L0_rec_w0': _L0_rec_in['w0'], 'L0_rec_w1': _L0_rec_in['w1'], 'L0_rec_w2': _L0_rec_in['w2'], 'L0_rec_b0': _L0_rec_in['b0'], 'L0_rec_b1': _L0_rec_in['b1'], 'L0_rec_b2': _L0_rec_in['b2']}

def reference(dense_ctx, ids, tbl_0, tbl_1, tbl_2, tbl_3, tbl_4, tbl_5, tbl_6, tbl_7, tbl_8, tbl_9, tbl_10, tbl_11, tbl_12, tbl_13, tbl_14, tbl_15, tbl_16, tbl_17, tbl_18, tbl_19, tbl_20, tbl_21, tbl_22, tbl_23, tbl_24, tbl_25, tbl_26, tbl_27, tbl_28, tbl_29, tbl_30, tbl_31, tbl_32, tbl_33, tbl_34, tbl_35, tbl_36, tbl_37, tbl_38, W_top1, b_top1, W_top2, b_top2, W_top3, L0_rec_w0, L0_rec_w1, L0_rec_w2, L0_rec_b0, L0_rec_b1, L0_rec_b2):
    import jax
    import jax.numpy as jnp

    def _L0_rec_ref(inputs, w0, w1, w2, b0, b1, b2):
        import jax, jax.numpy as jnp
        import numpy as np
        B, F0, D = (256, 39, 16)
        LAYER_SIZES = [128, 128, 128]
        x0 = inputs
        xk = inputs
        params = [(w0, b0), (w1, b1), (w2, b2)]
        n_layers = len(params)
        direct = []
        for idx, (W, b) in enumerate(params):
            z = jnp.einsum('bhd,bkd,hks->bsd', x0, xk, W) + b[None, :, None]
            z = jax.nn.relu(z)
            if idx != n_layers - 1:
                half = z.shape[1] // 2
                xk = z[:, :half, :]
                direct.append(z[:, half:, :])
            else:
                direct.append(z)
        logit = jnp.sum(jnp.concatenate(direct, axis=1), axis=-1)
        return logit
    e = jnp.stack([tbl_0[ids[:, 0]], tbl_1[ids[:, 1]], tbl_2[ids[:, 2]], tbl_3[ids[:, 3]], tbl_4[ids[:, 4]], tbl_5[ids[:, 5]], tbl_6[ids[:, 6]], tbl_7[ids[:, 7]], tbl_8[ids[:, 8]], tbl_9[ids[:, 9]], tbl_10[ids[:, 10]], tbl_11[ids[:, 11]], tbl_12[ids[:, 12]], tbl_13[ids[:, 13]], tbl_14[ids[:, 14]], tbl_15[ids[:, 15]], tbl_16[ids[:, 16]], tbl_17[ids[:, 17]], tbl_18[ids[:, 18]], tbl_19[ids[:, 19]], tbl_20[ids[:, 20]], tbl_21[ids[:, 21]], tbl_22[ids[:, 22]], tbl_23[ids[:, 23]], tbl_24[ids[:, 24]], tbl_25[ids[:, 25]], tbl_26[ids[:, 26]], tbl_27[ids[:, 27]], tbl_28[ids[:, 28]], tbl_29[ids[:, 29]], tbl_30[ids[:, 30]], tbl_31[ids[:, 31]], tbl_32[ids[:, 32]], tbl_33[ids[:, 33]], tbl_34[ids[:, 34]], tbl_35[ids[:, 35]], tbl_36[ids[:, 36]], tbl_37[ids[:, 37]], tbl_38[ids[:, 38]]], axis=1)
    z = _L0_rec_ref(e, L0_rec_w0, L0_rec_w1, L0_rec_w2, L0_rec_b0, L0_rec_b1, L0_rec_b2)
    z = z.reshape(z.shape[0], -1)
    h = jnp.concatenate([z, dense_ctx], axis=1)
    h = jnp.maximum(h @ W_top1 + b_top1, 0.0)
    h = jnp.maximum(h @ W_top2 + b_top2, 0.0)
    y = h @ W_top3
    return y

_drawn_inputs = setup_inputs


def setup_inputs(seed=0):
    import zlib

    import numpy as np

    out = dict(_drawn_inputs(seed))
    spreads = {'b_top1': (0.0, 2.0),
     'b_top2': (0.0, 2.0),
     'L0_rec_b0': (0.0, 0.348),
     'L0_rec_b1': (0.0, 0.53),
     'L0_rec_b2': (0.0, 0.8)}
    factors = {'tbl_0': 8.0,
     'tbl_1': 8.0,
     'tbl_2': 8.0,
     'tbl_3': 8.0,
     'tbl_4': 8.0,
     'tbl_5': 8.0,
     'tbl_6': 8.0,
     'tbl_7': 8.0,
     'tbl_8': 8.0,
     'tbl_9': 8.0,
     'tbl_10': 8.0,
     'tbl_11': 8.0,
     'tbl_12': 8.0,
     'tbl_13': 8.0,
     'tbl_14': 8.0,
     'tbl_15': 8.0,
     'tbl_16': 8.0,
     'tbl_17': 8.0,
     'tbl_18': 8.0,
     'tbl_19': 8.0,
     'tbl_20': 8.0,
     'tbl_21': 8.0,
     'tbl_22': 8.0,
     'tbl_23': 8.0,
     'tbl_24': 8.0,
     'tbl_25': 8.0,
     'tbl_26': 8.0,
     'tbl_27': 8.0,
     'tbl_28': 8.0,
     'tbl_29': 8.0,
     'tbl_30': 8.0,
     'tbl_31': 8.0,
     'tbl_32': 8.0,
     'tbl_33': 8.0,
     'tbl_34': 8.0,
     'tbl_35': 8.0,
     'tbl_36': 8.0,
     'tbl_37': 8.0,
     'tbl_38': 8.0,
     'L0_rec_w0': 8.0,
     'L0_rec_w1': 6.198,
     'L0_rec_w2': 4.842,
     'dense_ctx': 8.0}
    for name, (base, spread) in spreads.items():
        noise = np.random.default_rng([zlib.crc32(name.encode()), seed]).standard_normal(out[name].shape)
        drawn = base * np.exp(spread * noise) if base else spread * noise
        out[name] = jnp.asarray(drawn.astype(out[name].dtype))
    for name, factor in factors.items():
        out[name] = (out[name] * factor).astype(out[name].dtype)
    return out
```

```python
from contextlib import ExitStack

import concourse.bass as bass
from concourse import mybir


def cin_tower(nc: bass.Bass, ids, tables, dense, w_cin0, w_cin1, w_cin2, b_cin, w_top1, b_top1, w_top2, b_top2,
              w_top3, y_out):
    fp32 = mybir.dt.float32
    int32 = mybir.dt.int32
    ALU = mybir.AluOpType
    ACT = mybir.ActivationFunctionType
    P = 128

    BATCH, FIELDS = ids.shape
    DIM = tables[0].shape[1]
    NDENSE = dense.shape[1]
    BLOCKS = BATCH // P
    TILES = 4
    TD = DIM // TILES
    COLS = TD * P
    HALF = 64
    C0 = w_cin0.shape[2]
    U0 = 3
    R0 = U0 * FIELDS
    C1 = w_cin1.shape[1]
    WRAP = U0 * (C0 - 1) + U0 - 1 + FIELDS
    H1 = w_top1.shape[1]
    H2 = w_top2.shape[1]

    GROUP = 4
    def groups_of(layer):
        if layer == 0:
            return [(0, c, min(GROUP, C0 - c), False) for c in range(0, C0, GROUP)]
        return [(layer, c, min(GROUP, C1 - 1 - c), c + GROUP == C1) for c in range(0, C1, GROUP)]
    G0, G1, G2 = groups_of(0), groups_of(1), groups_of(2)
    STEP_GROUPS = len(G1) + len(G0) + len(G2)
    RING = 3
    assert STEP_GROUPS % RING == 0

    x_dram = nc.dram_tensor("x_transposed", [BLOCKS, WRAP, DIM * P], fp32)

    ctx = ExitStack()
    with ctx:
        def sb(name, shape, dt=fp32):
            return ctx.enter_context(nc.sbuf_tensor(name, shape, dt))

        def ps(name):
            return ctx.enter_context(nc.psum_tensor(name, [P, 512], fp32))

        def sem(name):
            return ctx.enter_context(nc.semaphore(name))

        w0 = sb("w0", [P, C0, P])
        w1 = sb("w1", [P, C1, P])
        w2 = sb("w2", [P, C1, P])
        bias = sb("bias", [P, 3])
        ident = sb("ident", [P, P])
        ids_sb = sb("ids_sb", [P, BLOCKS, FIELDS], int32)
        idx = sb("idx", [P, FIELDS], int32)
        emb = sb("emb", [P, FIELDS, DIM])
        xT = sb("xT", [2 * FIELDS, DIM * P // 2])
        x3 = sb("x3", [P, COLS])
        xroll = sb("xroll", [P, C0, COLS])
        xbc = sb("xbc", [P, 2, C1, COLS])
        xk = [sb("xk1", [P, COLS]), sb("xk2", [P, COLS])]
        prod = sb("prod", [P, RING, GROUP, COLS])
        d01 = sb("d01", [P, TILES, COLS])
        d2 = sb("d2", [P, TILES, COLS])
        s01 = sb("s01", [P, BATCH])
        s2 = sb("s2", [P, BATCH])

        wt1 = xbc[:, 0, 0:2, :]
        wt1d = xbc[0:NDENSE, 0, 2, :]
        wt2 = xbc[:, 0, 3:5, :].rearrange("p a (b n) -> p (a b) n", n=H2)
        wt3 = xbc[:, 0, 5, 0:2]
        bt1 = xbc[:, 0, 6, 0:4]
        bt2 = xbc[:, 0, 7, 0:2]
        dn = xbc[:, 0, 8, 0:BLOCKS * NDENSE].rearrange("p (i n) -> p i n", n=NDENSE)
        dnT = xbc[0:NDENSE, 0, 9:13, :].rearrange("p a n -> p (a n)")
        h1 = prod[:, 0, :, :]
        h2 = prod[:, 1, 0:2, :]
        y_sb = xbc[0:1, 0, 13:17, :].rearrange("p a n -> p (a n)")

        z = [ps("z0"), ps("z1"), ps("z2")]
        tp = [ps("tp0"), ps("tp1")]
        ph = [ps("ph0"), ps("ph1"), ps("ph2")]

        ids_in = sem("ids_in")
        w_in = sem("w_in")
        ident_ok = sem("ident_ok")
        w0_ready = sem("w0_ready")
        idx_ready = sem("idx_ready")
        gathered = sem("gathered")
        transposed = sem("transposed")
        xT_ready = sem("xT_ready")
        xT_saved = sem("xT_saved")
        l0_in = sem("l0_in")
        xbc_in = [sem("xbc_in0"), sem("xbc_in1")]
        prod_ready = sem("prod_ready")
        prod_used = sem("prod_used")
        z_read = [sem("z0_read"), sem("z1_read"), sem("z2_read")]
        xk_ready = [sem("xk1_ready"), sem("xk2_ready")]
        folds = sem("folds")
        ident_zero = sem("ident_zero")
        mlp_in = sem("mlp_in")
        dnT_ps = sem("dnT_ps")
        dnT_ready = sem("dnT_ready")
        h1_ps = sem("h1_ps")
        h1_ready = sem("h1_ready")
        h2_ps = sem("h2_ps")
        h2_ready = sem("h2_ready")
        y_ps = sem("y_ps")
        y_ready = sem("y_ready")
        y_out_done = sem("y_out_done")

        block = ctx.enter_context(nc.Block())

        L0_LOADS = 2 * U0
        XBC_LOADS = 2
        XT_BANKS = 2
        XT_SAVES = 2
        W_LOADS = 6
        def group_no(g, k):
            return g * STEP_GROUPS + (len(G0) + k)

        ADDS = 10

        def folds_at(i, k):
            return ADDS * (i + 1) + k + 1

        def slot_of(t, k):
            return (t * STEP_GROUPS + len(G0) + k) % RING

        @block.sync
        def _(sp):
            def load_l0(i, t):
                for u in range(U0):
                    rows = slice(u * FIELDS, (u + 1) * FIELDS)
                    src = x_dram[i, 0:FIELDS, t * COLS:(t + 1) * COLS]
                    sp.dma_start(x3[rows, :], src).then_inc(l0_in, 16)
                    first = x_dram[i, u:u + FIELDS, t * COLS:(t + 1) * COLS]
                    row = DIM * P
                    rolled = bass.AP(first.tensor, first.offset, [[row, FIELDS], [U0 * row, C0], [1, COLS]])
                    sp.dma_start(xroll[rows, :, :], rolled).then_inc(l0_in, 16)

            def load_xbc(i, t):
                for a in range(2):
                    n = C1 - a
                    first = x_dram[i, a:a + 1, t * COLS:(t + 1) * COLS]
                    src = bass.AP(first.tensor, first.offset, [[0, HALF], [2 * DIM * P, n], [1, COLS]])
                    sp.dma_start(xbc[a * HALF:(a + 1) * HALF, t % 2, 0:n, :], src).then_inc(xbc_in[t % 2], 16)

            def save_xT(i):
                sp.wait_ge(xT_ready, (i + 1) * XT_BANKS)
                rows = x_dram[i, :, :].rearrange("f (a n) -> (f a) n", a=2)
                n = 2 * (WRAP - FIELDS)
                sp.dma_start(rows[0:2 * FIELDS, :], xT[:, :]).then_inc(xT_saved, 16)
                sp.dma_start(rows[2 * FIELDS:2 * WRAP, :], xT[0:n, :]).then_inc(xT_saved, 16)

            sp.dma_start(ids_sb[:, :, :], ids.rearrange("(i p) f -> p i f", p=P)).then_inc(ids_in, 16)
            sp.dma_start(w0[0:R0, :, :], w_cin0[0, :, :, :]).then_inc(w_in, 16)
            sp.dma_start(prod[0:R0, 0, 0:2, :].rearrange("p a n -> p (a n)")[:, 0:C0 * P],
                         w_cin0[1, :, :, :].rearrange("p c s -> p (c s)")).then_inc(w_in, 16)
            sp.dma_start(w1[:, :, :], w_cin1).then_inc(w_in, 16)
            sp.dma_start(w2[:, :, :], w_cin2).then_inc(w_in, 16)
            sp.dma_start(bias[:, :], b_cin).then_inc(w_in, 16)
            sp.dma_start(s01[0:1, 0:1], b_cin[0:1, 0:1]).then_inc(w_in, 16)
            save_xT(0)
            sp.wait_ge(xT_saved, XT_SAVES * 16)
            load_l0(0, 0)
            load_xbc(0, 0)

            def step(i, t, last):
                g = i * TILES + t
                if not (last and t == TILES - 1):
                    if t == TILES - 1:
                        sp.wait_ge(xT_saved, (i + 2) * XT_SAVES * 16)
                    sp.wait_ge(prod_ready, group_no(g, 0))
                    load_l0(i + (t + 1) // TILES, (t + 1) % TILES)
                    load_xbc(i + (t + 1) // TILES, (t + 1) % TILES)
                if t == 1 and not last:
                    save_xT(i + 1)

            with sp.Fori(0, BLOCKS - 1) as i:
                for t in range(TILES):
                    step(i, t, False)
            for t in range(TILES):
                step(BLOCKS - 1, t, True)

            sp.wait_ge(prod_ready, group_no(BLOCKS * TILES - 2, STEP_GROUPS))
            with nc.allow_non_contiguous_dma(reason="small bias and weight columns"):
                sp.dma_start(wt1, w_top1[0:2 * P, :].rearrange("(a p) n -> p a n", p=P)).then_inc(mlp_in, 16)
                sp.dma_start(wt1d, w_top1[2 * P:2 * P + NDENSE, :]).then_inc(mlp_in, 16)
                sp.dma_start(wt2, w_top2.rearrange("(a p) n -> p a n", p=P)).then_inc(mlp_in, 16)
                sp.dma_start(wt3, w_top3).then_inc(mlp_in, 16)
                sp.dma_start(bt1, b_top1).then_inc(mlp_in, 16)
                sp.dma_start(bt2, b_top2).then_inc(mlp_in, 16)
                sp.dma_start(dn, dense.rearrange("(i p) n -> p i n", p=P)).then_inc(mlp_in, 16)
            sp.wait_ge(y_ready, BATCH // COLS)
            sp.dma_start(y_out.rearrange("b o -> o b"), y_sb).then_inc(y_out_done, 16)
            sp.wait_ge(y_out_done, 16)
        MLP_LOADS = 7

        @block.gpsimd
        def _(pool):
            nc.gpsimd.memset(ident[:, :], 0.0).then_inc(ident_zero, 1)
            pool.wait_ge(ident_zero, 1)
            nc.gpsimd.affine_select(out=ident[:, :], in_=ident[:, :], compare_op=ALU.not_equal, fill=1.0, base=0,
                                    pattern=[[-1, P]], channel_multiplier=1).then_inc(ident_ok, 1)
            nc.gpsimd.memset(idx[:, :], 0).then_inc(folds, ADDS)
            pool.wait_ge(folds, ADDS)
            pool.wait_ge(ids_in, 16)

            def stage_ids(i):
                nc.gpsimd.tensor_copy(idx[:, :], ids_sb[:, i, :]).then_inc(idx_ready, 1)

            def gather(fields):
                for f in fields:
                    nc.gpsimd.indirect_dma_start(
                        out=emb[:, f, :], out_offset=None, in_=tables[f],
                        in_offset=bass.IndirectOffsetOnAxis(ap=idx[:, f:f + 1], axis=0)).then_inc(gathered, 16)

            def add(i, k, out, a, b):
                pool.wait_ge(folds, folds_at(i, k - 1))
                nc.gpsimd.tensor_tensor(out, a, b, ALU.add).then_inc(folds, 1)

            def fold_tile(i, t, staged=None):
                if staged is not None:
                    pool.wait_ge(idx_ready, staged)
                pool.wait_ge(z_read[2], i * TILES + t + 2)
                for n, d in enumerate((d01, d2)):
                    add(i, 2 * (t - 1) + n, d[:, t, :], d[:, t - 1, :], d[:, t, :])

            def fold_block(i):
                e = TILES - 1
                for n, (d, s) in enumerate(((d01, s01), (d2, s2))):
                    add(i, 6 + 2 * n, d[:, e, 0:COLS // 2], d[:, e, 0:COLS // 2], d[:, e, COLS // 2:COLS])
                    add(i, 7 + 2 * n, s[:, bass.ds(i * P, P)], d[:, e, 0:P], d[:, e, P:2 * P])

            half = FIELDS // 2
            stage_ids(0)
            pool.wait_ge(idx_ready, 1)
            gather(range(FIELDS))
            pool.wait_ge(transposed, XT_BANKS)
            stage_ids(1)
            pool.wait_ge(idx_ready, 2)
            gather(range(FIELDS))

            def body(i, fetch):
                if fetch:
                    pool.wait_ge(transposed, (i + 2) * XT_BANKS)
                    stage_ids(i + 2)
                    fold_tile(i, 1, staged=i + 3)
                    gather(range(half))
                else:
                    fold_tile(i, 1)
                fold_tile(i, 2)
                if fetch:
                    gather(range(half, FIELDS))
                fold_tile(i, 3)
                fold_block(i)

            with pool.Fori(0, BLOCKS - 2) as i:
                body(i, True)
            body(BLOCKS - 2, False)
            body(BLOCKS - 1, False)

        @block.scalar
        def _(act):
            def save_transposed(i, t):
                act.wait_ge(transposed, i * XT_BANKS + t + 1)
                nc.scalar.activation(xT[:, t * 512:(t + 1) * 512], tp[t][0:2 * FIELDS, :], ACT.Copy).then_inc(xT_ready, 1)

            def feed(layer, t, d, rows, n):
                act.wait_ge(prod_used, n + 1)
                for a in range(2):
                    nc.scalar.activation(xk[layer][a * HALF:(a + 1) * HALF, :], z[layer][0:HALF, :], ACT.Relu,
                                         bias=bias[0:HALF, layer:layer + 1]).then_inc(xk_ready[layer], 1)
                nc.scalar.activation(d[rows, t, :], z[layer][HALF:P, :], ACT.Relu,
                                     bias=bias[HALF:P, layer:layer + 1]).then_inc(z_read[layer], 1)

            for layer in range(3):
                act.nop().then_inc(z_read[layer], 1)
            act.wait_ge(w_in, W_LOADS * 16)
            for t in range(XT_BANKS):
                save_transposed(0, t)
            feed(0, 0, d01, slice(0, HALF), len(G0))

            def step(i, t, last):
                g = i * TILES + t
                k = len(G1)
                feed(1, t, d01, slice(HALF, P), group_no(g, k))
                if t == 1 and not last:
                    act.wait_ge(xT_saved, (i + 1) * XT_SAVES * 16)
                    for n in range(XT_BANKS):
                        save_transposed(i + 1, n)
                if not (last and t == TILES - 1):
                    k += len(G0)
                    if t < TILES - 1:
                        act.wait_ge(folds, folds_at(i - 1, (3, 5, 9)[t]))
                    else:
                        act.wait_ge(folds, folds_at(i, 1))
                    feed(0, (t + 1) % TILES, d01, slice(0, HALF), group_no(g, k))
                k += len(G2)
                act.wait_ge(prod_used, group_no(g, k) + 1)
                nc.scalar.activation(d2[:, t, :], z[2][:, :], ACT.Relu, bias=bias[:, 2:3]).then_inc(z_read[2], 1)

            with act.Fori(0, BLOCKS - 1) as i:
                for t in range(TILES):
                    step(i, t, False)
            for t in range(TILES):
                step(BLOCKS - 1, t, True)

            act.wait_ge(dnT_ps, 1)
            act.wait_ge(mlp_in, MLP_LOADS * 16)
            for n in range(4):
                nc.scalar.activation(dnT[:, n * COLS:(n + 1) * COLS], (tp + ph)[n][0:NDENSE, :],
                                     ACT.Copy).then_inc(dnT_ready, 1)
            for n in range(BATCH // COLS):
                for m in range(H1 // P):
                    act.wait_ge(h1_ps, n * 4 + m + 1)
                    nc.scalar.activation(h1[:, m, :], (z + tp)[m][:, :], ACT.Relu,
                                         bias=bt1[:, m:m + 1]).then_inc(h1_ready, 1)
                for m in range(H2 // P):
                    act.wait_ge(h2_ps, n * 2 + m + 1)
                    nc.scalar.activation(h2[:, m, :], ph[m][:, :], ACT.Relu,
                                         bias=bt2[:, m:m + 1]).then_inc(h2_ready, 1)
                act.wait_ge(y_ps, n + 1)
                nc.scalar.activation(y_sb[:, n * COLS:(n + 1) * COLS], ph[2][0:1, :],
                                     ACT.Copy).then_inc(y_ready, 1)

        @block.vector
        def _(dve):
            dve.wait_ge(w_in, W_LOADS * 16)
            w0b = prod[0:R0, 0, 0:2, :].rearrange("p a n -> p (a n)")[:, 0:C0 * P]
            w0a = w0[0:R0, :, :].rearrange("p c s -> p (c s)")
            nc.vector.tensor_tensor(w0a, w0a, w0b, ALU.add).then_inc(w0_ready, 1)
            dve.wait_ge(w0_ready, 1)

            def multiply(group, slot, xk_ap, x_ap, rows):
                _, c, n, half = group
                dst = prod[0:rows, slot, 0:n, :]
                last = nc.vector.tensor_tensor(dst, xk_ap[0:rows, :].unsqueeze(1).to_broadcast([rows, n, COLS]),
                                               x_ap[0:rows, c:c + n, :], ALU.mult)
                if half:
                    last = nc.vector.tensor_tensor(prod[0:HALF, slot, n, :], xk_ap[0:HALF, :],
                                                   x_ap[0:HALF, c + n, :], ALU.mult)
                last.then_inc(prod_ready, 1)

            def step(i, t, last):
                g = i * TILES + t
                k = 0
                for layer in (1, 0, 2):
                    if layer == 0 and last and t == TILES - 1:
                        continue
                    if layer == 0:
                        dve.wait_ge(l0_in, (g + 2) * L0_LOADS * 16)
                    elif layer == 1:
                        dve.wait_ge(xbc_in[t % 2], (i * (TILES // 2) + t // 2 + 1) * XBC_LOADS * 16)
                        dve.wait_ge(xk_ready[0], 2 * (g + 1))
                    else:
                        dve.wait_ge(xk_ready[1], 2 * (g + 1))
                    for group in (G0, G1, G2)[layer]:
                        dve.wait_ge(prod_used, group_no(g, k) + 2 - RING)
                        if layer == 0:
                            multiply(group, slot_of(t, k), x3, xroll, R0)
                        else:
                            multiply(group, slot_of(t, k), xk[layer - 1], xbc[:, t % 2, :, :], P)
                        k += 1

            dve.wait_ge(l0_in, L0_LOADS * 16)
            for k, group in enumerate(G0):
                multiply(group, k, x3, xroll, R0)
            with dve.Fori(0, BLOCKS - 1) as i:
                for t in range(TILES):
                    step(i, t, False)
            for t in range(TILES):
                step(BLOCKS - 1, t, True)

        @block.tensor
        def _(pe):
            def transpose_block(i):
                pe.wait_ge(gathered, (i + 1) * FIELDS * 16)
                if not isinstance(i, int):
                    pe.wait_ge(xT_ready, i * XT_BANKS)
                for t in range(XT_BANKS):
                    for d in range(4):
                        dims = slice(t * 4 + d, FIELDS * DIM, DIM // 2)
                        last = nc.tensor.transpose(tp[t][0:2 * FIELDS, d * P:(d + 1) * P],
                                                   emb[:, :, :].rearrange("p f d -> p (f d)")[:, dims], ident[:, :])
                    last.then_inc(transposed, 1)

            def contract(group, slot, z_ap, w_ap, rows, chunks, n):
                _, c, full, half = group
                pe.wait_ge(prod_ready, n + 1)
                for j in range(full + half):
                    r = HALF if half and j == full else rows
                    last = nc.tensor.matmul(z_ap[:, :], w_ap[0:r, c + j, :], prod[0:r, slot, j, :],
                                            start=(c + j == 0), stop=(c + j == chunks - 1))
                last.then_inc(prod_used, 1)

            def step(i, t, last):
                g = i * TILES + t
                k = 0
                for layer in (1, 0, 2):
                    if layer == 0 and last and t == TILES - 1:
                        continue
                    if layer == 0:
                        pe.wait_ge(z_read[0], g + 2)
                    else:
                        pe.wait_ge(z_read[layer], g + 1)
                    for group in (G0, G1, G2)[layer]:
                        contract(group, slot_of(t, k), z[layer], (w0, w1, w2)[layer],
                                       R0 if layer == 0 else P, C0 if layer == 0 else C1, group_no(g, k))
                        k += 1
                    if layer == 1 and t == 1 and not last:
                        transpose_block(i + 1)

            pe.nop().then_inc(prod_used, 1)
            pe.wait_ge(ident_ok, 1)
            transpose_block(0)
            pe.wait_ge(w_in, W_LOADS * 16)
            pe.wait_ge(w0_ready, 1)
            for k, group in enumerate(G0):
                contract(group, k, z[0], w0, R0, C0, k)
            with pe.Fori(0, BLOCKS - 1) as i:
                for t in range(TILES):
                    step(i, t, False)
            for t in range(TILES):
                step(BLOCKS - 1, t, True)

            pe.wait_ge(mlp_in, MLP_LOADS * 16)
            for i in range(BLOCKS):
                last = nc.tensor.transpose((tp + ph)[i // 4][0:NDENSE, (i % 4) * P:(i % 4 + 1) * P], dn[:, i, :],
                                           ident[:, :])
            last.then_inc(dnT_ps, 1)
            pe.wait_ge(dnT_ready, 4)
            pe.wait_ge(z_read[2], BLOCKS * TILES + 1)
            pe.wait_ge(folds, folds_at(BLOCKS - 1, ADDS - 1))
            for n in range(BATCH // COLS):
                cols = slice(n * COLS, (n + 1) * COLS)
                for m in range(H1 // P):
                    if n > 0:
                        pe.wait_ge(h1_ready, (n - 1) * 4 + m + 1)
                    rows = slice(m * P, (m + 1) * P)
                    nc.tensor.matmul((z + tp)[m][:, :], wt1[:, 0, rows], s01[:, cols], start=True, stop=False)
                    nc.tensor.matmul((z + tp)[m][:, :], wt1[:, 1, rows], s2[:, cols], start=False, stop=False)
                    nc.tensor.matmul((z + tp)[m][:, :], wt1d[:, rows], dnT[:, cols], start=False,
                                     stop=True).then_inc(h1_ps, 1)
                for m in range(H2 // P):
                    pe.wait_ge(h1_ready, (n + 1) * 4)
                    if n > 0:
                        pe.wait_ge(h2_ready, (n - 1) * 2 + m + 1)
                    for k in range(H1 // P):
                        last = nc.tensor.matmul(ph[m][:, :], wt2[:, k, m * P:(m + 1) * P], h1[:, k, :],
                                                start=(k == 0), stop=(k == H1 // P - 1))
                    last.then_inc(h2_ps, 1)
                pe.wait_ge(h2_ready, (n + 1) * 2)
                if n > 0:
                    pe.wait_ge(y_ready, n)
                for k in range(H2 // P):
                    last = nc.tensor.matmul(ph[2][0:1, :], wt3[:, k:k + 1], h2[:, k, :],
                                            start=(k == 0), stop=(k == H2 // P - 1))
                last.then_inc(y_ps, 1)


def kernel(**inputs):
    import numpy as np
    import concourse.bacc as bacc
    from concourse import mybir as mb
    from concourse.bass_utils import run_bass_kernel_spmd

    f32 = np.float32
    w0, w1, w2 = (np.asarray(inputs[f"L0_rec_w{n}"]) for n in range(3))
    fields, _, size = w0.shape
    u0 = 3
    c0 = (fields // 2 + 1 + u0 - 1) // u0
    w_cin0 = np.zeros((2, u0 * fields, c0, size), f32)
    for c in range(c0):
        for u in range(u0):
            r = u0 * c + u
            if r <= fields // 2:
                i = np.arange(fields)
                j = (i + r) % fields
                w_cin0[0, u * fields:(u + 1) * fields, c] = w0[i, j]
                if r > 0:
                    w_cin0[1, u * fields:(u + 1) * fields, c] = w0[j, i]

    def pairs(w):
        h, k, s = w.shape
        full = np.zeros((h + h % 2, k, s), f32)
        full[:h] = w
        return np.ascontiguousarray(full.reshape(-1, 2, k, s).transpose(1, 2, 0, 3).reshape(2 * k, -1, s))

    a = {
        "ids": np.asarray(inputs["ids"]),
        "dense": np.asarray(inputs["dense_ctx"]),
        "w_cin0": w_cin0, "w_cin1": pairs(w1), "w_cin2": pairs(w2),
        "b_cin": np.stack([np.asarray(inputs[f"L0_rec_b{n}"]) for n in range(3)], axis=1),
        "w_top1": np.asarray(inputs["W_top1"]),
        "b_top1": np.asarray(inputs["b_top1"]).reshape(-1, 128).T,
        "w_top2": np.asarray(inputs["W_top2"]),
        "b_top2": np.asarray(inputs["b_top2"]).reshape(-1, 128).T,
        "w_top3": np.asarray(inputs["W_top3"]).reshape(-1, 128).T,
    }
    for f in range(fields):
        a[f"tbl_{f}"] = np.asarray(inputs[f"tbl_{f}"])
    a = {name: np.ascontiguousarray(v) for name, v in a.items()}

    nc = bacc.Bacc("TRN2", target_bir_lowering=False, num_devices=1)
    ap = {name: nc.dram_tensor(name, v.shape, mb.dt.from_np(v.dtype), kind="ExternalInput").ap()
          for name, v in a.items()}
    batch = a["ids"].shape[0]
    y = nc.dram_tensor("y", (batch, 1), mb.dt.float32, kind="ExternalOutput").ap()
    cin_tower(nc, ap["ids"], [ap[f"tbl_{f}"] for f in range(fields)], ap["dense"], ap["w_cin0"], ap["w_cin1"],
              ap["w_cin2"], ap["b_cin"], ap["w_top1"], ap["b_top1"], ap["w_top2"], ap["b_top2"], ap["w_top3"], y)
    r = run_bass_kernel_spmd(nc, [a], core_ids=[0])
    return r.results[0]["y"]
```

```python
from contextlib import ExitStack

import concourse.bass as bass
from concourse import mybir


def cin_tower(nc: bass.Bass, ids, tables, dense, w_cin0, w_cin1, w_cin2, b_cin, w_top1, b_top1, w_top2, b_top2,
              w_top3, y_out):
    fp32 = mybir.dt.float32
    fp32r = mybir.dt.float32r
    int32 = mybir.dt.int32
    ALU = mybir.AluOpType
    ACT = mybir.ActivationFunctionType
    P = 128

    BATCH, FIELDS = ids.shape
    DIM = tables[0].shape[1]
    NDENSE = dense.shape[1]
    BLOCKS = BATCH // P
    TILES = 4
    TD = DIM // TILES
    COLS = TD * P
    HALF = 64
    C0 = w_cin0.shape[2]
    U0 = 3
    R0 = U0 * FIELDS
    C1 = w_cin1.shape[1]
    WRAP = U0 * (C0 - 1) + U0 - 1 + FIELDS
    H1 = w_top1.shape[1]
    H2 = w_top2.shape[1]

    S, L = True, False
    UNITS0 = [(S, 0, 2, 0), (S, 2, 2, 0), (L, 4, 3, 0)]
    UNITS1 = [(S, 0, 2, 0), (L, 8, 3, 0), (S, 2, 2, 0), (L, 11, 3, 0), (S, 4, 2, 0), (L, 14, 3, 0), (S, 6, 2, 0),
              (L, 17, 2, 1)]
    UNITS = [UNITS0, UNITS1, UNITS1]
    CHUNKS = [C0, C1, C1]
    SPLIT_CHUNKS = [sum(n for split, _, n, _ in u if split) for u in UNITS]
    ROWS = [R0, P, P]
    def count(kind, *layers):
        return sum(unit[0] == kind for layer in layers for unit in UNITS[layer])
    ORDER = (1, 0, 2)
    STEP_SPLIT, STEP_PLAIN = count(S, 0, 1, 2), count(L, 0, 1, 2)
    RING = 2
    SPLIT_N, PLAIN_N = 2, 3
    assert STEP_SPLIT * TILES % RING == 0 and STEP_PLAIN * TILES % RING == 0

    x_dram = nc.dram_tensor("x_transposed", [BLOCKS, WRAP, DIM * P], fp32)

    s_dram = nc.dram_tensor("direct_sums", [BLOCKS, P, 2, P], fp32)

    ctx = ExitStack()
    with ctx:
        def sb(name, shape, dt=fp32):
            return ctx.enter_context(nc.sbuf_tensor(name, shape, dt))

        def ps(name):
            return ctx.enter_context(nc.psum_tensor(name, [P, 512], fp32))

        def sem(name):
            return ctx.enter_context(nc.semaphore(name))

        w = [sb(f"w{n}", [P, CHUNKS[n] - SPLIT_CHUNKS[n], P]) for n in range(3)]
        w_hi = [sb(f"w{n}_hi", [P, SPLIT_CHUNKS[n], P], fp32r) for n in range(3)]
        w_lo = [sb(f"w{n}_lo", [P, SPLIT_CHUNKS[n], P], fp32r) for n in range(3)]
        bias = sb("bias", [P, 3])
        ident = sb("ident", [P, P])
        ids_sb = sb("ids_sb", [P, BLOCKS, FIELDS], int32)
        idx = sb("idx", [P, FIELDS], int32)
        emb = sb("emb", [P, FIELDS, DIM])
        xT = sb("xT", [2 * FIELDS, DIM * P // 2])
        x3 = sb("x3", [P, COLS])
        xroll = sb("xroll", [P, C0, COLS])
        xbc = sb("xbc", [P, 2, C1, COLS])
        prod = sb("prod", [P, RING, PLAIN_N, COLS])
        sprod = sb("sprod", [P, RING, SPLIT_N, COLS])
        p_hi = sb("p_hi", [P, RING, SPLIT_N, COLS], fp32r)
        p_lo = sb("p_lo", [P, RING, SPLIT_N, COLS], fp32r)
        d01 = sb("d01", [P, TILES, COLS])
        d2 = sb("d2", [P, TILES, COLS])
        s_blk = sb("s_blk", [P, 2, P])

        staged, at = [], 0
        for n in range(3):
            staged.append(xbc[:, 1, :, :].rearrange("p c n -> p (c n)")[:, at * P:(at + SPLIT_CHUNKS[n]) * P]
                          .rearrange("p (c s) -> p c s", s=P))
            at += SPLIT_CHUNKS[n]
        w0_swapped = xbc[:, 1, :, :].rearrange("p c n -> p (c n)")[:, at * P:(at + C0) * P]\
            .rearrange("p (c s) -> p c s", s=P)

        wt1 = xbc[:, 0, 0:2, :]
        wt1d = xbc[0:NDENSE, 0, 2, :]
        wt2 = xbc[:, 0, 3:5, :].rearrange("p a (b n) -> p (a b) n", n=H2)
        wt3 = xbc[:, 0, 5, 0:2]
        bt1 = xbc[:, 0, 5, 2:6]
        bt2 = xbc[:, 0, 5, 6:8]
        dn = xbc[:, 0, 5, 8:8 + BLOCKS * NDENSE].rearrange("p (i n) -> p i n", n=NDENSE)
        dnT = xbc[0:NDENSE, 0, 6:10, :].rearrange("p a n -> p (a n)")
        s01 = xbc[:, 0, 10:14, :].rearrange("p a n -> p (a n)")
        s2 = xbc[:, 0, 14:18, :].rearrange("p a n -> p (a n)")
        h1 = d2
        h2 = prod[:, 0, 0:2, :]
        y_sb = d01[0:1, :, :].rearrange("p a n -> p (a n)")

        z = [ps("z0"), ps("z1"), ps("z2")]
        tp = [ps("tp0"), ps("tp1")]
        xk = [ps("xk1"), ps("xk2")]
        ph = [*xk, ps("ph2")]

        ids_in = sem("ids_in")
        w_in = sem("w_in")
        ident_ok = sem("ident_ok")
        w0_ready = sem("w0_ready")
        w_hi_ready = sem("w_hi_ready")
        w_lo_ready = sem("w_lo_ready")
        idx_ready = sem("idx_ready")
        gathered = sem("gathered")
        transposed = sem("transposed")
        xT_ready = sem("xT_ready")
        xT_saved = sem("xT_saved")
        l0_in = sem("l0_in")
        xbc_in = [sem("xbc_in0"), sem("xbc_in1")]
        plain_ready = sem("plain_ready")
        plain_used = sem("plain_used")
        sprod_ready = sem("sprod_ready")
        hi_ready = sem("hi_ready")
        lo_ready = sem("lo_ready")
        split_used = sem("split_used")
        s_saved = sem("s_saved")
        z_read = [sem("z0_read"), sem("z1_read"), sem("z2_read")]
        xk_ready = [sem("xk1_ready"), sem("xk2_ready")]
        folds = sem("folds")
        ident_zero = sem("ident_zero")
        mlp_in = sem("mlp_in")
        s_in = sem("s_in")
        dnT_ps = sem("dnT_ps")
        dnT_ready = sem("dnT_ready")
        h1_ps = sem("h1_ps")
        h1_ready = sem("h1_ready")
        h2_ps = sem("h2_ps")
        h2_ready = sem("h2_ready")
        y_ps = sem("y_ps")
        y_ready = sem("y_ready")
        y_out_done = sem("y_out_done")

        block = ctx.enter_context(nc.Block())

        L0_LOADS = 2 * U0
        XBC_LOADS = 2
        XT_BANKS = 2
        XT_SAVES = 2
        W_LOADS = 8
        def done(kind, g, *layers):
            return count(kind, 0) + g * (STEP_SPLIT if kind else STEP_PLAIN) + count(kind, *layers)

        def units_of(g, t, last):
            k = {S: 0, L: 0}
            for layer in ORDER:
                if layer == 0 and last and t == TILES - 1:
                    continue
                for unit in UNITS[layer]:
                    kind = unit[0]
                    per_step = STEP_SPLIT if kind else STEP_PLAIN
                    yield (layer, unit, done(kind, g) + k[kind], (count(kind, 0) + t * per_step + k[kind]) % RING)
                    k[kind] += 1

        def first_units():
            k = {S: 0, L: 0}
            for unit in UNITS[0]:
                yield 0, unit, k[unit[0]], k[unit[0]] % RING
                k[unit[0]] += 1

        ADDS = 10

        def folds_at(i, k):
            return ADDS * (i + 1) + k + 1

        @block.sync
        def _(sp):
            def load_l0(i, t):
                for u in range(U0):
                    rows = slice(u * FIELDS, (u + 1) * FIELDS)
                    src = x_dram[i, 0:FIELDS, t * COLS:(t + 1) * COLS]
                    sp.dma_start(x3[rows, :], src).then_inc(l0_in, 16)
                    first = x_dram[i, u:u + FIELDS, t * COLS:(t + 1) * COLS]
                    row = DIM * P
                    rolled = bass.AP(first.tensor, first.offset, [[row, FIELDS], [U0 * row, C0], [1, COLS]])
                    sp.dma_start(xroll[rows, :, :], rolled).then_inc(l0_in, 16)

            def load_xbc(i, t):
                for a in range(2):
                    n = C1 - a
                    first = x_dram[i, a:a + 1, t * COLS:(t + 1) * COLS]
                    src = bass.AP(first.tensor, first.offset, [[0, HALF], [2 * DIM * P, n], [1, COLS]])
                    sp.dma_start(xbc[a * HALF:(a + 1) * HALF, t % 2, 0:n, :], src).then_inc(xbc_in[t % 2], 16)

            def save_xT(i):
                sp.wait_ge(xT_ready, (i + 1) * XT_BANKS)
                rows = x_dram[i, :, :].rearrange("f (a n) -> (f a) n", a=2)
                n = 2 * (WRAP - FIELDS)
                sp.dma_start(rows[0:2 * FIELDS, :], xT[:, :]).then_inc(xT_saved, 16)
                sp.dma_start(rows[2 * FIELDS:2 * WRAP, :], xT[0:n, :]).then_inc(xT_saved, 16)

            sp.dma_start(ids_sb[:, :, :], ids.rearrange("(i p) f -> p i f", p=P)).then_inc(ids_in, 16)
            for n, src in enumerate((w_cin0[0], w_cin1, w_cin2)):
                r = ROWS[n]
                sp.dma_start(staged[n][0:r, :, :], src[:, 0:SPLIT_CHUNKS[n], :]).then_inc(w_in, 16)
                sp.dma_start(w[n][0:r, :, :], src[:, SPLIT_CHUNKS[n]:CHUNKS[n], :]).then_inc(w_in, 16)
            sp.dma_start(w0_swapped[0:R0, :, :], w_cin0[1]).then_inc(w_in, 16)
            sp.dma_start(bias[:, :], b_cin).then_inc(w_in, 16)
            save_xT(0)
            sp.wait_ge(xT_saved, XT_SAVES * 16)
            load_l0(0, 0)
            load_xbc(0, 0)

            def step(i, t, last):
                g = i * TILES + t
                if not (last and t == TILES - 1):
                    if t == TILES - 1:
                        sp.wait_ge(xT_saved, (i + 2) * XT_SAVES * 16)
                    sp.wait_ge(plain_ready, done(L, g))
                    if t == 0:
                        sp.wait_ge(w_lo_ready, 3)
                    load_l0(i + (t + 1) // TILES, (t + 1) % TILES)
                    load_xbc(i + (t + 1) // TILES, (t + 1) % TILES)
                if t == 1 and not last:
                    save_xT(i + 1)

            with sp.Fori(0, BLOCKS - 1) as i:
                for t in range(TILES):
                    step(i, t, False)
            for t in range(TILES):
                step(BLOCKS - 1, t, True)

            sp.wait_ge(plain_ready, done(L, BLOCKS * TILES - 1))
            with nc.allow_non_contiguous_dma(reason="small bias and weight columns"):
                sp.dma_start(wt1, w_top1[0:2 * P, :].rearrange("(a p) n -> p a n", p=P)).then_inc(mlp_in, 16)
                sp.dma_start(wt1d, w_top1[2 * P:2 * P + NDENSE, :]).then_inc(mlp_in, 16)
                sp.dma_start(wt2, w_top2.rearrange("(a p) n -> p a n", p=P)).then_inc(mlp_in, 16)
                sp.dma_start(wt3, w_top3).then_inc(mlp_in, 16)
                sp.dma_start(bt1, b_top1).then_inc(mlp_in, 16)
                sp.dma_start(bt2, b_top2).then_inc(mlp_in, 16)
                sp.dma_start(dn, dense.rearrange("(i p) n -> p i n", p=P)).then_inc(mlp_in, 16)
            sp.wait_ge(s_saved, BLOCKS * 16)
            for n, s in enumerate((s01, s2)):
                sp.dma_start(s.rearrange("p (i n) -> p i n", n=P),
                             s_dram[:, :, n, :].rearrange("i p n -> p i n")).then_inc(s_in, 16)
            sp.wait_ge(y_ready, BATCH // COLS)
            sp.dma_start(y_out.rearrange("b o -> o b"), y_sb).then_inc(y_out_done, 16)
            sp.wait_ge(y_out_done, 16)
        MLP_LOADS = 7

        @block.gpsimd
        def _(pool):
            nc.gpsimd.memset(ident[:, :], 0.0).then_inc(ident_zero, 1)
            pool.wait_ge(ident_zero, 1)
            nc.gpsimd.affine_select(out=ident[:, :], in_=ident[:, :], compare_op=ALU.not_equal, fill=1.0, base=0,
                                    pattern=[[-1, P]], channel_multiplier=1).then_inc(ident_ok, 1)
            nc.gpsimd.memset(idx[:, :], 0).then_inc(folds, ADDS)
            pool.wait_ge(folds, ADDS)
            pool.wait_ge(ids_in, 16)

            def stage_ids(i):
                nc.gpsimd.tensor_copy(idx[:, :], ids_sb[:, i, :]).then_inc(idx_ready, 1)

            def gather(fields):
                for f in fields:
                    nc.gpsimd.indirect_dma_start(
                        out=emb[:, f, :], out_offset=None, in_=tables[f],
                        in_offset=bass.IndirectOffsetOnAxis(ap=idx[:, f:f + 1], axis=0)).then_inc(gathered, 16)

            def add(i, k, out, a, b):
                pool.wait_ge(folds, folds_at(i, k - 1))
                nc.gpsimd.tensor_tensor(out, a, b, ALU.add).then_inc(folds, 1)

            def fold_tile(i, t, staged=None):
                if staged is not None:
                    pool.wait_ge(idx_ready, staged)
                pool.wait_ge(z_read[2], i * TILES + t + 2)
                for n, d in enumerate((d01, d2)):
                    add(i, 2 * (t - 1) + n, d[:, t, :], d[:, t - 1, :], d[:, t, :])

            def fold_block(i):
                e = TILES - 1
                for n, d in enumerate((d01, d2)):
                    add(i, 6 + 2 * n, d[:, e, 0:COLS // 2], d[:, e, 0:COLS // 2], d[:, e, COLS // 2:COLS])
                    add(i, 7 + 2 * n, s_blk[:, n, :], d[:, e, 0:P], d[:, e, P:2 * P])

                pool.wait_ge(folds, folds_at(i, ADDS - 1))
                nc.gpsimd.dma_start(s_dram[i, :, :, :], s_blk[:, :, :]).then_inc(s_saved, 16)
                pool.wait_ge(s_saved, (i + 1) * 16)

            half = FIELDS // 2
            stage_ids(0)
            pool.wait_ge(idx_ready, 1)
            gather(range(FIELDS))
            pool.wait_ge(transposed, XT_BANKS)
            stage_ids(1)
            pool.wait_ge(idx_ready, 2)
            gather(range(FIELDS))

            def body(i, fetch):
                if fetch:
                    pool.wait_ge(transposed, (i + 2) * XT_BANKS)
                    stage_ids(i + 2)
                    fold_tile(i, 1, staged=i + 3)
                    gather(range(half))
                else:
                    fold_tile(i, 1)
                fold_tile(i, 2)
                if fetch:
                    gather(range(half, FIELDS))
                fold_tile(i, 3)
                fold_block(i)

            with pool.Fori(0, BLOCKS - 2) as i:
                body(i, True)
            body(BLOCKS - 2, False)
            body(BLOCKS - 1, False)

        @block.scalar
        def _(act):
            def save_transposed(i, t):
                act.wait_ge(transposed, i * XT_BANKS + t + 1)
                nc.scalar.activation(xT[:, t * 512:(t + 1) * 512], tp[t][0:2 * FIELDS, :], ACT.Copy).then_inc(xT_ready, 1)

            def feed(layer, t, d, rows, n):
                act.wait_ge(plain_used, n + 1)
                for a in range(2):
                    nc.scalar.activation(xk[layer][a * HALF:(a + 1) * HALF, :], z[layer][0:HALF, :], ACT.Relu,
                                         bias=bias[0:HALF, layer:layer + 1]).then_inc(xk_ready[layer], 1)
                nc.scalar.activation(d[rows, t, :], z[layer][HALF:P, :], ACT.Relu,
                                     bias=bias[HALF:P, layer:layer + 1]).then_inc(z_read[layer], 1)

            for layer in range(3):
                act.nop().then_inc(z_read[layer], 1)
            act.wait_ge(w_in, W_LOADS * 16)
            act.wait_ge(w0_ready, 2)
            for n in range(3):
                r = ROWS[n]
                nc.scalar.activation(w_hi[n][0:r, :, :], staged[n][0:r, :, :], ACT.Copy).then_inc(w_hi_ready, 1)
            for t in range(XT_BANKS):
                save_transposed(0, t)

            def round_high(rows, number, buf, first):
                act.wait_ge(sprod_ready, number + 1)
                if not first:
                    act.wait_ge(split_used, number + 1 - RING)
                nc.scalar.activation(p_hi[0:rows, buf, :, :], sprod[0:rows, buf, :, :],
                                     ACT.Copy).then_inc(hi_ready, 1)

            for _, unit, number, buf in first_units():
                if unit[0]:
                    round_high(R0, number, buf, True)
            feed(0, 0, d01, slice(0, HALF), count(L, 0))

            AHEAD = RING

            def step(i, t, last):
                g = i * TILES + t
                more = not (last and t == TILES - 1)
                splits = {layer: [u[1:] for u in units_of(g, t, last) if u[0] == layer and u[1][0]]
                          for layer in ORDER}
                for _, number, buf in splits[1][AHEAD:]:
                    round_high(P, number, buf, False)
                for _, number, buf in splits[0]:
                    round_high(R0, number, buf, False)
                feed(1, t, d01, slice(HALF, P), done(L, g, 1))
                if t == 1 and not last:
                    act.wait_ge(xT_saved, (i + 1) * XT_SAVES * 16)
                    for n in range(XT_BANKS):
                        save_transposed(i + 1, n)
                for k, (_, number, buf) in enumerate(splits[2]):
                    if k == AHEAD and more:
                        feed0(i, t, g)
                    round_high(P, number, buf, False)
                if more:
                    rounds_ahead(g + 1, t + 1)
                act.wait_ge(plain_used, (done(L, g, 1, 0, 2) if more else done(L, g, 1, 2)) + 1)
                nc.scalar.activation(d2[:, t, :], z[2][:, :], ACT.Relu, bias=bias[:, 2:3]).then_inc(z_read[2], 1)

            def rounds_ahead(g, t):
                ahead = [u for u in units_of(g, t, False) if u[1][0]][:AHEAD]
                for _, _, number, buf in ahead:
                    round_high(P, number, buf, False)

            def feed0(i, t, g):
                if t < TILES - 1:
                    act.wait_ge(folds, folds_at(i - 1, (3, 5, 9)[t]))
                else:
                    act.wait_ge(folds, folds_at(i, 1))
                feed(0, (t + 1) % TILES, d01, slice(0, HALF), done(L, g, 1, 0))

            rounds_ahead(0, 0)
            with act.Fori(0, BLOCKS - 1) as i:
                for t in range(TILES):
                    step(i, t, False)
            for t in range(TILES):
                step(BLOCKS - 1, t, True)

            act.wait_ge(dnT_ps, 1)
            act.wait_ge(mlp_in, MLP_LOADS * 16)
            for n in range(4):
                nc.scalar.activation(dnT[:, n * COLS:(n + 1) * COLS], (tp + ph)[n][0:NDENSE, :],
                                     ACT.Copy).then_inc(dnT_ready, 1)
            for n in range(BATCH // COLS):
                for m in range(H1 // P):
                    act.wait_ge(h1_ps, n * 4 + m + 1)
                    nc.scalar.activation(h1[:, m, :], (z + tp)[m][:, :], ACT.Relu,
                                         bias=bt1[:, m:m + 1]).then_inc(h1_ready, 1)
                for m in range(H2 // P):
                    act.wait_ge(h2_ps, n * 2 + m + 1)
                    nc.scalar.activation(h2[:, m, :], ph[m][:, :], ACT.Relu,
                                         bias=bt2[:, m:m + 1]).then_inc(h2_ready, 1)
                act.wait_ge(y_ps, n + 1)
                nc.scalar.activation(y_sb[:, n * COLS:(n + 1) * COLS], ph[2][0:1, :],
                                     ACT.Copy).then_inc(y_ready, 1)

        @block.vector
        def _(dve):
            dve.wait_ge(w_in, W_LOADS * 16)
            n = SPLIT_CHUNKS[0]
            for part, cs in ((staged[0], slice(0, n)), (w[0], slice(n, C0))):
                nc.vector.tensor_tensor(part[0:R0, :, :], part[0:R0, :, :], w0_swapped[0:R0, cs, :],
                                        ALU.add).then_inc(w0_ready, 1)
            for n in range(3):
                r = ROWS[n]
                dve.wait_ge(w_hi_ready, n + 1)
                nc.vector.tensor_tensor(w_lo[n][0:r, :, :], staged[n][0:r, :, :], w_hi[n][0:r, :, :],
                                        ALU.subtract).then_inc(w_lo_ready, 1)

            def multiply(layer, unit, number, buf, t):
                split, c, n, half = unit
                rows = ROWS[layer]
                x_ap = xroll if layer == 0 else xbc[:, t % 2, :, :]
                xk_ap = x3 if layer == 0 else xk[layer - 1]
                ring, ready = (sprod, sprod_ready) if split else (prod, plain_ready)
                last = nc.vector.tensor_tensor(ring[0:rows, buf, 0:n, :],
                                               xk_ap[0:rows, :].unsqueeze(1).to_broadcast([rows, n, COLS]),
                                               x_ap[0:rows, c:c + n, :], ALU.mult)
                if half:
                    last = nc.vector.tensor_tensor(ring[0:HALF, buf, n, :], xk_ap[0:HALF, :],
                                                   x_ap[0:HALF, c + n, :], ALU.mult)
                last.then_inc(ready, 1)

            def subtract_high(layer, number, buf, first):
                rows = ROWS[layer]
                dve.wait_ge(hi_ready, number + 1)
                if not first:
                    dve.wait_ge(split_used, number + 1 - RING)
                nc.vector.tensor_tensor(p_lo[0:rows, buf, :, :], sprod[0:rows, buf, :, :],
                                        p_hi[0:rows, buf, :, :], ALU.subtract).then_inc(lo_ready, 1)

            def run(units, t, before_layer, first=False):
                pending, layer_now = None, None
                for layer, unit, number, buf in units:
                    if layer != layer_now:
                        before_layer(layer)
                        layer_now = layer
                    if not unit[0] and not first:
                        dve.wait_ge(plain_used, number + 2 - RING)
                    if unit[0] and not first:
                        dve.wait_ge(lo_ready, number + 1 - RING)
                    multiply(layer, unit, number, buf, t)
                    if pending is not None:
                        subtract_high(*pending)
                    pending = (layer, number, buf, first) if unit[0] else None
                assert pending is None

            def step(i, t, last):
                g = i * TILES + t

                def before_layer(layer):
                    if layer == 0:
                        dve.wait_ge(l0_in, (g + 2) * L0_LOADS * 16)
                    else:
                        if layer == 1:
                            dve.wait_ge(xbc_in[t % 2], (i * (TILES // 2) + t // 2 + 1) * XBC_LOADS * 16)
                        dve.wait_ge(xk_ready[layer - 1], 2 * (g + 1))

                run(units_of(g, t, last), t, before_layer)

            run(first_units(), 0, lambda layer: dve.wait_ge(l0_in, L0_LOADS * 16), first=True)
            with dve.Fori(0, BLOCKS - 1) as i:
                for t in range(TILES):
                    step(i, t, False)
            for t in range(TILES):
                step(BLOCKS - 1, t, True)

        @block.tensor
        def _(pe):
            def transpose_block(i):
                pe.wait_ge(gathered, (i + 1) * FIELDS * 16)
                if not isinstance(i, int):
                    pe.wait_ge(xT_ready, i * XT_BANKS)
                for t in range(XT_BANKS):
                    for d in range(4):
                        dims = slice(t * 4 + d, FIELDS * DIM, DIM // 2)
                        last = nc.tensor.transpose(tp[t][0:2 * FIELDS, d * P:(d + 1) * P],
                                                   emb[:, :, :].rearrange("p f d -> p (f d)")[:, dims], ident[:, :])
                    last.then_inc(transposed, 1)

            def contract(layer, unit, number, buf):
                split, c, full, half = unit
                pe.wait_ge(lo_ready if split else plain_ready, number + 1)
                for j in range(full + half):
                    ch = c + j
                    r = HALF if j == full else ROWS[layer]
                    start, stop = ch == 0, ch == CHUNKS[layer] - 1
                    if split:
                        hi, lo = p_hi[0:r, buf, j, :], p_lo[0:r, buf, j, :]
                        nc.tensor.matmul(z[layer][:, :], w_hi[layer][0:r, ch, :], hi, start=start, stop=False)
                        nc.tensor.matmul(z[layer][:, :], w_hi[layer][0:r, ch, :], lo, start=False, stop=False)
                        last = nc.tensor.matmul(z[layer][:, :], w_lo[layer][0:r, ch, :], hi, start=False, stop=stop)
                    else:
                        last = nc.tensor.matmul(z[layer][:, :], w[layer][0:r, ch - SPLIT_CHUNKS[layer], :],
                                                prod[0:r, buf, j, :], start=start, stop=stop)
                last.then_inc(split_used if split else plain_used, 1)

            def step(i, t, last):
                g = i * TILES + t
                layer_now = None
                for layer, unit, number, buf in units_of(g, t, last):
                    if layer != layer_now:
                        pe.wait_ge(z_read[layer], g + 2 if layer == 0 else g + 1)
                    if layer_now == 1 and layer != 1 and t == 1 and not last:
                        transpose_block(i + 1)
                    layer_now = layer
                    contract(layer, unit, number, buf)

            pe.nop().then_inc(plain_used, 1)
            pe.wait_ge(ident_ok, 1)
            transpose_block(0)
            pe.wait_ge(w_lo_ready, 3)
            for u in first_units():
                contract(*u)
            with pe.Fori(0, BLOCKS - 1) as i:
                for t in range(TILES):
                    step(i, t, False)
            for t in range(TILES):
                step(BLOCKS - 1, t, True)

            pe.wait_ge(mlp_in, MLP_LOADS * 16)
            for i in range(BLOCKS):
                last = nc.tensor.transpose((tp + ph)[i // 4][0:NDENSE, (i % 4) * P:(i % 4 + 1) * P], dn[:, i, :],
                                           ident[:, :])
            last.then_inc(dnT_ps, 1)
            pe.wait_ge(dnT_ready, 4)
            pe.wait_ge(z_read[2], BLOCKS * TILES + 1)
            pe.wait_ge(s_in, 32)
            for n in range(BATCH // COLS):
                cols = slice(n * COLS, (n + 1) * COLS)
                for m in range(H1 // P):
                    if n > 0:
                        pe.wait_ge(h1_ready, (n - 1) * 4 + m + 1)
                    rows = slice(m * P, (m + 1) * P)
                    nc.tensor.matmul((z + tp)[m][:, :], wt1[:, 0, rows], s01[:, cols], start=True, stop=False)
                    nc.tensor.matmul((z + tp)[m][:, :], wt1[:, 1, rows], s2[:, cols], start=False, stop=False)
                    nc.tensor.matmul((z + tp)[m][:, :], wt1d[:, rows], dnT[:, cols], start=False,
                                     stop=True).then_inc(h1_ps, 1)
                for m in range(H2 // P):
                    pe.wait_ge(h1_ready, (n + 1) * 4)
                    if n > 0:
                        pe.wait_ge(h2_ready, (n - 1) * 2 + m + 1)
                    for k in range(H1 // P):
                        last = nc.tensor.matmul(ph[m][:, :], wt2[:, k, m * P:(m + 1) * P], h1[:, k, :],
                                                start=(k == 0), stop=(k == H1 // P - 1))
                    last.then_inc(h2_ps, 1)
                pe.wait_ge(h2_ready, (n + 1) * 2)
                if n > 0:
                    pe.wait_ge(y_ready, n)
                for k in range(H2 // P):
                    last = nc.tensor.matmul(ph[2][0:1, :], wt3[:, k:k + 1], h2[:, k, :],
                                            start=(k == 0), stop=(k == H2 // P - 1))
                last.then_inc(y_ps, 1)


def kernel(**inputs):
    import numpy as np
    import concourse.bacc as bacc
    from concourse import mybir as mb
    from concourse.bass_utils import run_bass_kernel_spmd

    f32 = np.float32
    w0, w1, w2 = (np.asarray(inputs[f"L0_rec_w{n}"]) for n in range(3))
    fields, _, size = w0.shape
    u0 = 3
    c0 = (fields // 2 + 1 + u0 - 1) // u0
    w_cin0 = np.zeros((2, u0 * fields, c0, size), f32)
    for c in range(c0):
        for u in range(u0):
            r = u0 * c + u
            if r <= fields // 2:
                i = np.arange(fields)
                j = (i + r) % fields
                w_cin0[0, u * fields:(u + 1) * fields, c] = w0[i, j]
                if r > 0:
                    w_cin0[1, u * fields:(u + 1) * fields, c] = w0[j, i]

    def pairs(w):
        h, k, s = w.shape
        full = np.zeros((h + h % 2, k, s), f32)
        full[:h] = w
        return np.ascontiguousarray(full.reshape(-1, 2, k, s).transpose(1, 2, 0, 3).reshape(2 * k, -1, s))

    a = {
        "ids": np.asarray(inputs["ids"]),
        "dense": np.asarray(inputs["dense_ctx"]),
        "w_cin0": w_cin0, "w_cin1": pairs(w1), "w_cin2": pairs(w2),
        "b_cin": np.stack([np.asarray(inputs[f"L0_rec_b{n}"]) for n in range(3)], axis=1),
        "w_top1": np.asarray(inputs["W_top1"]),
        "b_top1": np.asarray(inputs["b_top1"]).reshape(-1, 128).T,
        "w_top2": np.asarray(inputs["W_top2"]),
        "b_top2": np.asarray(inputs["b_top2"]).reshape(-1, 128).T,
        "w_top3": np.asarray(inputs["W_top3"]).reshape(-1, 128).T,
    }
    for f in range(fields):
        a[f"tbl_{f}"] = np.asarray(inputs[f"tbl_{f}"])
    a = {name: np.ascontiguousarray(v) for name, v in a.items()}

    nc = bacc.Bacc("TRN2", target_bir_lowering=False, num_devices=1)
    ap = {name: nc.dram_tensor(name, v.shape, mb.dt.from_np(v.dtype), kind="ExternalInput").ap()
          for name, v in a.items()}
    batch = a["ids"].shape[0]
    y = nc.dram_tensor("y", (batch, 1), mb.dt.float32, kind="ExternalOutput").ap()
    cin_tower(nc, ap["ids"], [ap[f"tbl_{f}"] for f in range(fields)], ap["dense"], ap["w_cin0"], ap["w_cin1"],
              ap["w_cin2"], ap["b_cin"], ap["w_top1"], ap["b_top1"], ap["w_top2"], ap["b_top2"], ap["w_top3"], y)
    r = run_bass_kernel_spmd(nc, [a], core_ids=[0])
    return r.results[0]["y"]
```

```python
from contextlib import ExitStack

import concourse.bass as bass
from concourse import mybir


def cin_tower(nc: bass.Bass, ids, tables, dense, w_cin0, w_cin1, w_cin2, b_cin, w_top1, b_top1, w_top2, b_top2,
              w_top3, y_out):
    fp32 = mybir.dt.float32
    fp32r = mybir.dt.float32r
    int32 = mybir.dt.int32
    ALU = mybir.AluOpType
    ACT = mybir.ActivationFunctionType
    P = 128

    BATCH, FIELDS = ids.shape
    DIM = tables[0].shape[1]
    NDENSE = dense.shape[1]
    BLOCKS = BATCH // P
    TILES = 4
    TD = DIM // TILES
    COLS = TD * P
    HALF = 64
    C0 = w_cin0.shape[2]
    U0 = 3
    R0 = U0 * FIELDS
    C1 = w_cin1.shape[1]
    WRAP = U0 * (C0 - 1) + U0 - 1 + FIELDS
    H1 = w_top1.shape[1]
    H2 = w_top2.shape[1]

    S, L = True, False
    UNITS0 = [(S, 0, 2, 0), (S, 2, 2, 0), (S, 4, 2, 0), (L, 6, 1, 0)]
    UNITS2A = [(S, 0, 2, 0), (L, 14, 2, 0), (S, 2, 2, 0), (L, 16, 2, 0), (S, 4, 2, 0), (L, 18, 1, 1)]
    UNITS2B = [(S, 6, 2, 0), (L, 8, 2, 0), (L, 10, 2, 0), (L, 12, 2, 0)]
    UNITS1 = UNITS2A + [(S, 6, 2, 0), (L, 10, 2, 0), (S, 8, 2, 0), (L, 12, 2, 0)]
    LATE = slice(6, 14)
    UNITS = [UNITS0, UNITS1, UNITS2A + UNITS2B]
    CHUNKS = [C0, C1, C1]
    SPLIT_CHUNKS = [sum(n for split, _, n, _ in u if split) for u in UNITS]
    ROWS = [R0, P, P]
    SPREAD = (2, 3, 4, 6, 7, 11, 11)
    SPREAD_FIRST = (3, 4, 4, 5, 5, 5, 5)
    ORDER = ((2, UNITS2A), (1, UNITS1), (2, UNITS2B))
    P_RING, S_RING = 4, 2
    SPLIT_N, PLAIN_N = 2, 2

    def count(split, *pieces):
        return sum(unit[0] == split for n in pieces for unit in ORDER[n][1])
    assert count(S, 0, 1, 2) * TILES % S_RING == 0 and count(L, 0, 1, 2) * TILES % P_RING == 0

    x_dram = nc.dram_tensor("x_transposed", [BLOCKS, WRAP, DIM * P], fp32)
    pairs_dram = nc.dram_tensor("x_pairs", [BLOCKS, TILES, 2, C1, COLS], fp32)

    s_dram = nc.dram_tensor("direct_sums", [BLOCKS, P, 2, P], fp32)

    ctx = ExitStack()
    with ctx:
        def sb(name, shape, dt=fp32):
            return ctx.enter_context(nc.sbuf_tensor(name, shape, dt))

        def ps(name):
            return ctx.enter_context(nc.psum_tensor(name, [P, 512], fp32))

        def sem(name):
            return ctx.enter_context(nc.semaphore(name))

        w = [sb(f"w{n}", [P, CHUNKS[n] - SPLIT_CHUNKS[n], P]) for n in range(3)]
        w_hi = [sb(f"w{n}_hi", [P, SPLIT_CHUNKS[n], P], fp32r) for n in range(3)]
        w_lo = [sb(f"w{n}_lo", [P, SPLIT_CHUNKS[n], P], fp32r) for n in range(3)]
        bias = sb("bias", [P, 3])
        ident = sb("ident", [P, P])
        idx = sb("idx", [P, FIELDS], int32)
        emb = sb("emb", [P, FIELDS, DIM])
        xT = sb("xT", [2 * FIELDS, DIM * P // 2])
        x3 = sb("x3", [P, COLS])
        xroll = sb("xroll", [P, C0, COLS])
        xbc = sb("xbc", [P, 2, C1, COLS])
        prod0 = sb("prod0", [P, 1, COLS])
        sprod0 = sb("sprod0", [P, SPLIT_N, COLS])
        p0_hi = sb("p0_hi", [P, 2, SPLIT_N, COLS], fp32r)
        p0_lo = sb("p0_lo", [P, 2, SPLIT_N, COLS], fp32r)
        prod = sb("prod", [P, P_RING, PLAIN_N, COLS])
        p_hi = sb("p_hi", [P, S_RING, SPLIT_N, COLS], fp32r)
        p_lo = sb("p_lo", [P, S_RING, SPLIT_N, COLS], fp32r)
        d01 = sb("d01", [P, TILES, COLS])
        d2 = sb("d2", [P, 2, COLS])


        staged, at = [], 0
        for n in range(3):
            staged.append(xbc[:, 1, :, :].rearrange("p c n -> p (c n)")[:, at * P:(at + SPLIT_CHUNKS[n]) * P]
                          .rearrange("p (c s) -> p c s", s=P))
            at += SPLIT_CHUNKS[n]
        w0_swapped = xbc[:, 1, :, :].rearrange("p c n -> p (c n)")[:, at * P:(at + C0) * P]\
            .rearrange("p (c s) -> p c s", s=P)

        wt1 = xbc[:, 0, 0:2, :]
        wt1d = xbc[0:NDENSE, 0, 2, :]
        wt2 = xbc[:, 0, 3:5, :].rearrange("p a (b n) -> p (a b) n", n=H2)
        wt3 = xbc[:, 0, 5, 0:2]
        bt1 = xbc[:, 0, 5, 2:6]
        bt2 = xbc[:, 0, 5, 6:8]
        dn = xbc[:, 0, 5, 8:8 + BLOCKS * NDENSE].rearrange("p (i n) -> p i n", n=NDENSE)
        dnT = xbc[0:NDENSE, 0, 6:10, :].rearrange("p a n -> p (a n)")
        s01 = xbc[:, 0, 10:14, :].rearrange("p a n -> p (a n)")
        s2 = xbc[:, 0, 14:18, :].rearrange("p a n -> p (a n)")
        h1 = xroll[:, 0:4, :]
        h2 = xroll[:, 4:6, :]
        y_sb = d01[0:1, :, :].rearrange("p a n -> p (a n)")

        z0, z1, z2 = [ps("z0_0"), ps("z0_1")], [ps("z1_0"), ps("z1_1")], ps("z2")
        tp = ps("tp")
        sprod = ctx.enter_context(nc.psum_tensor("sprod", [P, SPLIT_N, COLS], fp32))
        h1_bank, h2_bank, y_bank = [tp, z0[0], z0[1], z1[0]], [z1[1], z2], sprod[:, 0, :]

        w_in = sem("w_in")
        ident_ok = sem("ident_ok")
        w0_ready = sem("w0_ready")
        w_hi_ready = sem("w_hi_ready")
        w_lo_ready = sem("w_lo_ready")
        idx_in = sem("idx_in")
        gathered = sem("gathered")
        transposed = sem("transposed")
        direct_read = [sem("direct0_read"), sem("direct1_read")]
        xT_ready = sem("xT_ready")
        xT_saved = sem("xT_saved")
        pairs_saved = sem("pairs_saved")
        l0_in = sem("l0_in")
        early_in = [sem("early_in0"), sem("early_in1")]
        late_in = [sem("late_in0"), sem("late_in1")]
        sprod0_ready = sem("sprod0_ready")
        hi0_ready = sem("hi0_ready")
        lo0_ready = sem("lo0_ready")
        prod0_ready = sem("prod0_ready")
        l0_used = sem("l0_used")
        plain_ready = sem("plain_ready")
        plain_used = sem("plain_used")
        sprod_ready = sem("sprod_ready")
        hi_ready = sem("hi_ready")
        lo_ready = sem("lo_ready")
        split_used = sem("split_used")
        s_saved = sem("s_saved")
        xk_ready = [sem("xk1_ready"), sem("xk2_ready")]
        z2_read = sem("z2_read")
        folds = sem("folds")
        ident_zero = sem("ident_zero")
        mlp_in = sem("mlp_in")
        s_in = sem("s_in")
        dnT_ps = sem("dnT_ps")
        dnT_ready = sem("dnT_ready")
        h1_ps = sem("h1_ps")
        h1_ready = sem("h1_ready")
        h2_ps = sem("h2_ps")
        h2_ready = sem("h2_ready")
        y_ps = sem("y_ps")
        y_ready = sem("y_ready")
        y_out_done = sem("y_out_done")

        block = ctx.enter_context(nc.Block())

        L0_LOADS = 1 + U0
        EARLY_LOADS, LATE_LOADS = 2, 1
        XT_HALVES = 2
        XT_SAVES, PAIR_SAVES = 2, 5
        W_LOADS = 8
        N0, S0 = len(UNITS0), sum(split for split, *_ in UNITS0)
        LAST = BLOCKS * TILES - 1
        RING0 = 2

        def buf0(t, k):
            return (S0 * t + k) % RING0
        assert S0 * TILES % RING0 == 0

        def used0(g, k):
            return N0 * g + k - 1 if k >= RING0 else N0 * (g - 1) + S0 + k - 1

        def done(split, g, *pieces):
            return count(split, 1) + g * count(split, 0, 1, 2) + count(split, *pieces)

        class Unit:
            def __init__(self, layer, spec, number, buf):
                self.layer, self.number, self.buf = layer, number, buf
                self.split, self.chunk, self.full, self.half = spec
                self.late = LATE.start <= self.chunk < LATE.stop

        def units_of(g, t, piece, last=False):
            nth = {S: count(S, *range(piece)), L: count(L, *range(piece))}
            if last and t == TILES - 1 and piece == 2:
                nth = {S: count(S, 0), L: count(L, 0)}
            out = []
            for spec in ORDER[piece][1]:
                split = spec[0]
                buf = (count(split, 1) + t * count(split, 0, 1, 2) + nth[split]) % (S_RING if split else P_RING)
                out.append(Unit(ORDER[piece][0], spec, done(split, g) + nth[split], buf))
                nth[split] += 1
            return out

        def first_units():
            nth, out = {S: 0, L: 0}, []
            for spec in UNITS1:
                split = spec[0]
                out.append(Unit(1, spec, nth[split], nth[split] % (S_RING if split else P_RING)))
                nth[split] += 1
            return out

        ADDS = 10

        def folds_at(i, k):
            return ADDS * (i + 1) + k + 1

        def turn(i):
            return 1 if isinstance(i, int) and i == 0 else 0

        @block.sync
        def _(sp):
            row = DIM * P

            def load_l0(i, t):
                first = x_dram[i, 0:1, t * COLS:(t + 1) * COLS]
                thrice = bass.AP(first.tensor, first.offset, [[0, U0], [row, FIELDS], [1, COLS]])
                sp.dma_start(x3[0:R0, :], thrice).then_inc(l0_in, 16)
                for u in range(U0):
                    first = x_dram[i, u:u + 1, t * COLS:(t + 1) * COLS]
                    rolled = bass.AP(first.tensor, first.offset, [[row, FIELDS], [U0 * row, C0], [1, COLS]])
                    sp.dma_start(xroll[u * FIELDS:(u + 1) * FIELDS, :, :], rolled).then_inc(l0_in, 16)

            def load_xbc(i, t, chunks, loaded):
                c, n = chunks.start, chunks.stop - chunks.start
                first = pairs_dram[i, t, 0, c:c + 1, :]
                src = bass.AP(first.tensor, first.offset, [[C1 * COLS, 2], [0, HALF], [1, n * COLS]])
                sp.dma_start(xbc[:, t % 2, c:c + n, :].rearrange("p c n -> p (c n)"), src).then_inc(loaded[t % 2], 16)

            def load_early(i, t):
                load_xbc(i, t, slice(0, LATE.start), early_in)
                load_xbc(i, t, slice(LATE.stop, C1), early_in)

            def load_late(i, t):
                load_xbc(i, t, LATE, late_in)

            def save_rows(i):
                sp.wait_ge(xT_ready, (i + 1) * XT_HALVES)
                rows = x_dram[i, :, :].rearrange("f (a n) -> (f a) n", a=2)
                n = 2 * (WRAP - FIELDS)
                sp.dma_start(rows[0:2 * FIELDS, :], xT[:, :]).then_inc(xT_saved, 16)
                sp.dma_start(rows[2 * FIELDS:2 * WRAP, :], xT[0:n, :]).then_inc(xT_saved, 16)

            def save_pairs(i):
                tile = 2 * C1 * COLS
                for h in range(2):
                    for a in range(2):
                        n = C1 - a
                        first = pairs_dram[i, 2 * h, a, 0:1, :]
                        dst = bass.AP(first.tensor, first.offset, [[COLS, n], [tile, 2], [1, COLS]])
                        src = xT[2 * a + h:2 * FIELDS:4, :].rearrange("c (q n) -> c q n", q=2)
                        sp.dma_start(dst, src).then_inc(pairs_saved, 16)
                first = pairs_dram[i, 0, 1, C1 - 1:C1, :]
                dst = bass.AP(first.tensor, first.offset, [[2 * tile, 2], [tile, 2], [1, COLS]])
                sp.dma_start(dst, xT[0:2, :].rearrange("h (q n) -> h q n", q=2)).then_inc(pairs_saved, 16)

            def save_xT(i):
                save_rows(i)
                save_pairs(i)

            ids_blocks = ids.rearrange("(i p) f -> i p f", p=P)

            def load_ids(i):
                if not isinstance(i, int) or i > 0:
                    sp.wait_ge(gathered, i * FIELDS * 16)
                sp.dma_start(idx[:, :], ids_blocks[i, :, :]).then_inc(idx_in, 16)

            load_ids(0)
            for n, src in enumerate((w_cin0[0], w_cin1, w_cin2)):
                r = ROWS[n]
                sp.dma_start(staged[n][0:r, :, :], src[:, 0:SPLIT_CHUNKS[n], :]).then_inc(w_in, 16)
                sp.dma_start(w[n][0:r, :, :], src[:, SPLIT_CHUNKS[n]:CHUNKS[n], :]).then_inc(w_in, 16)
            sp.dma_start(w0_swapped[0:R0, :, :], w_cin0[1]).then_inc(w_in, 16)
            sp.dma_start(bias[:, :], b_cin).then_inc(w_in, 16)
            load_ids(1)
            save_rows(0)
            sp.wait_ge(xT_saved, XT_SAVES * 16)
            load_l0(0, 0)
            save_pairs(0)
            sp.wait_ge(pairs_saved, PAIR_SAVES * 16)
            load_early(0, 0)
            sp.wait_ge(sprod0_ready, S0)
            load_l0(0, 1)
            load_late(0, 0)
            sp.wait_ge(w_lo_ready, 3)
            load_early(0, 1)
            sp.wait_ge(sprod0_ready, 2 * S0)
            load_l0(0, 2)
            load_late(0, 1)

            def step(i, t, fetch, last):
                g = i * TILES + t
                if t == turn(i) and fetch:
                    load_ids(i + 2)
                if t == 1 and not last:
                    if turn(i) == 1:
                        save_xT(i + 1)
                    sp.wait_ge(xT_saved, (i + 2) * XT_SAVES * 16)
                if not (last and t + 3 >= TILES):
                    sp.wait_ge(sprod0_ready, S0 * (g + 3))
                    load_l0(i + (t + 3) // TILES, (t + 3) % TILES)
                if t == 2 and not last:
                    sp.wait_ge(pairs_saved, (i + 2) * PAIR_SAVES * 16)
                if not (last and t + 2 >= TILES):
                    sp.wait_ge(plain_ready, done(L, g, 0))
                    load_early(i + (t + 2) // TILES, (t + 2) % TILES)
                if t == 0 and turn(i) == 0 and not last:
                    save_xT(i + 1)
                if not (last and t + 2 >= TILES):
                    sp.wait_ge(plain_ready, done(L, g, 0, 1, 2))
                    load_late(i + (t + 2) // TILES, (t + 2) % TILES)

            for t in range(TILES):
                step(0, t, True, False)
            with sp.Fori(1, BLOCKS - 2) as i:
                for t in range(TILES):
                    step(i, t, True, False)
            for t in range(TILES):
                step(BLOCKS - 2, t, False, False)
            for t in range(TILES):
                step(BLOCKS - 1, t, False, True)

            sp.wait_ge(plain_ready, done(L, LAST - 1, 0, 1, 2))
            with nc.allow_non_contiguous_dma(reason="small bias and weight columns"):
                sp.dma_start(wt1, w_top1[0:2 * P, :].rearrange("(a p) n -> p a n", p=P)).then_inc(mlp_in, 16)
                sp.dma_start(wt1d, w_top1[2 * P:2 * P + NDENSE, :]).then_inc(mlp_in, 16)
                sp.dma_start(wt2, w_top2.rearrange("(a p) n -> p a n", p=P)).then_inc(mlp_in, 16)
                sp.dma_start(wt3, w_top3).then_inc(mlp_in, 16)
                sp.dma_start(bt1, b_top1).then_inc(mlp_in, 16)
                sp.dma_start(bt2, b_top2).then_inc(mlp_in, 16)
                sp.dma_start(dn, dense.rearrange("(i p) n -> p i n", p=P)).then_inc(mlp_in, 16)
            sp.wait_ge(s_saved, (BLOCKS - 1) * 2 * 16)
            n = BLOCKS - 1
            for k, s in enumerate((s01, s2)):
                sp.dma_start(s[:, 0:n * P].rearrange("p (i n) -> p i n", n=P),
                             s_dram[0:n, :, k, :].rearrange("i p n -> p i n")).then_inc(s_in, 16)
            for n in range(BATCH // COLS):
                sp.wait_ge(y_ready, n + 1)
                sp.dma_start(y_out[n * COLS:(n + 1) * COLS, :].rearrange("b o -> o b"),
                             y_sb[:, n * COLS:(n + 1) * COLS]).then_inc(y_out_done, 16)
            sp.wait_ge(y_out_done, BATCH // COLS * 16)
        MLP_LOADS = 7

        @block.gpsimd
        def _(pool):
            nc.gpsimd.memset(ident[:, :], 0.0).then_inc(ident_zero, 1)
            pool.wait_ge(ident_zero, 1)
            nc.gpsimd.affine_select(out=ident[:, :], in_=ident[:, :], compare_op=ALU.not_equal, fill=1.0, base=0,
                                    pattern=[[-1, P]], channel_multiplier=1).then_inc(ident_ok, 1)
            nc.gpsimd.memset(d01[:, TILES - 1, :], 0.0).then_inc(folds, ADDS)
            pool.wait_ge(folds, ADDS)

            def gather(fields):
                for f in fields:
                    nc.gpsimd.indirect_dma_start(
                        out=emb[:, f, :], out_offset=None, in_=tables[f],
                        in_offset=bass.IndirectOffsetOnAxis(ap=idx[:, f:f + 1], axis=0)).then_inc(gathered, 16)

            def add(i, k, out, a, b):
                pool.wait_ge(folds, folds_at(i, k - 1))
                nc.gpsimd.tensor_tensor(out, a, b, ALU.add).then_inc(folds, 1)

            def fold_tile(i, t):
                pool.wait_ge(z2_read, i * TILES + t + 2)
                for n, (old, new) in enumerate(((d01[:, t - 1, :], d01[:, t, :]), (d2[:, (t - 1) % 2, :], d2[:, t % 2, :]))):
                    add(i, 2 * (t - 1) + n, new, old, new)

            def fold_block(i, out=None):
                for n, d in enumerate(LAST_TILE):
                    add(i, 6 + 2 * n, d[:, 0:COLS // 2], d[:, 0:COLS // 2], d[:, COLS // 2:COLS])
                    add(i, 7 + 2 * n, d[:, 0:P] if out is None else out[n], d[:, 0:P], d[:, P:2 * P])
                if out is None:
                    pool.wait_ge(folds, folds_at(i, ADDS - 1))
                    for n, d in enumerate(LAST_TILE):
                        nc.gpsimd.dma_start(s_dram[i, :, n, :], d[:, 0:P]).then_inc(s_saved, 16)

            LAST_TILE = (d01[:, TILES - 1, :], d2[:, (TILES - 1) % 2, :])

            def layer0(g, t, before_low=None, between=None):
                def multiply(out, k, ready):
                    _, c, n, _ = UNITS0[k]
                    nc.gpsimd.tensor_tensor(out[0:R0, 0:n, :], x3[0:R0, :].unsqueeze(1).to_broadcast([R0, n, COLS]),
                                            xroll[0:R0, c:c + n, :], ALU.mult).then_inc(ready, 1)

                def subtract_high(k):
                    pool.wait_ge(l0_used, used0(g, k))
                    pool.wait_ge(hi0_ready, S0 * g + k + 1)
                    nc.gpsimd.tensor_tensor(p0_lo[0:R0, buf0(t, k), :, :], sprod0[0:R0, :, :],
                                            p0_hi[0:R0, buf0(t, k), :, :], ALU.subtract).then_inc(lo0_ready, 1)

                pool.wait_ge(l0_in, (g + 1) * L0_LOADS * 16)
                pool.wait_ge(lo0_ready, S0 * g)
                multiply(sprod0, 0, sprod0_ready)
                subtract_high(0)
                pool.wait_ge(lo0_ready, S0 * g + 1)
                multiply(sprod0, 1, sprod0_ready)
                if before_low:
                    before_low()
                subtract_high(1)
                pool.wait_ge(l0_used, N0 * g)
                multiply(prod0, 3, prod0_ready)
                pool.wait_ge(lo0_ready, S0 * g + 2)
                multiply(sprod0, 2, sprod0_ready)
                if between:
                    between()
                subtract_high(2)

            def body(i, before, fetch, last):
                shares = (3, 12, 12, 12) if turn(i) == 0 else (0, 7, 16, 16)
                assert sum(shares) == FIELDS
                for t in range(TILES):
                    def fetch_rows():
                        gather(range(sum(shares[:t]), sum(shares[:t + 1])))

                    def sums():
                        if t == 0 and before:
                            fold_tile(i - 1, TILES - 1)
                        elif t >= 2:
                            fold_tile(i, t - 1)
                        if t == turn(i) and fetch:
                            pool.wait_ge(transposed, (i + 2) * XT_HALVES)
                            pool.wait_ge(idx_in, (i + 3) * 16)
                        if t == 0 and before:
                            fold_block(i - 1)

                    if last and t + 2 >= TILES:
                        sums()
                    else:
                        filler = fetch_rows if fetch and t > turn(i) else None
                        if t == 0 and not before:
                            filler = lambda: gather(range(BLOCK1[0], BLOCK1[1]))
                        layer0(i * TILES + t + 2, t + 2, filler, sums)
                    if t == 0 and not before:
                        gather(range(BLOCK1[1], FIELDS))
                    if fetch and t == turn(i):
                        fetch_rows()

            BLOCK1 = (28, 34)
            pool.wait_ge(idx_in, 16)
            gather(range(FIELDS))
            pool.wait_ge(transposed, XT_HALVES)
            pool.wait_ge(idx_in, 32)
            gather(range(BLOCK1[0]))
            layer0(1, 1)

            body(0, False, True, False)
            with pool.Fori(1, BLOCKS - 2) as i:
                body(i, True, True, False)
            body(BLOCKS - 2, True, False, False)
            body(BLOCKS - 1, True, False, True)
            fold_tile(BLOCKS - 1, TILES - 1)
            pool.wait_ge(plain_ready, done(L, LAST - 1, 0, 1, 2))
            fold_block(BLOCKS - 1, [s[:, (BLOCKS - 1) * P:BLOCKS * P] for s in (s01, s2)])

        @block.scalar
        def _(act):
            def save_transposed(i, t):
                act.wait_ge(transposed, i * XT_HALVES + t + 1)
                nc.scalar.activation(xT[:, t * 512:(t + 1) * 512], tp[0:2 * FIELDS, :], ACT.Copy).then_inc(xT_ready, 1)

            def feed(layer, g, t, z, direct):
                nc.scalar.activation(d01[direct, t, :], z[HALF:P, :], ACT.Relu,
                                     bias=bias[HALF:P, layer:layer + 1]).then_inc(direct_read[layer], 1)
                act.wait_ge(direct_read[layer], g + 1)
                nc.scalar.activation(z[HALF:P, :], z[0:HALF, :], ACT.Relu,
                                     bias=bias[0:HALF, layer:layer + 1]).then_inc(xk_ready[layer], 1)
                act.wait_ge(xk_ready[layer], 2 * g + 1)
                nc.scalar.activation(z[0:HALF, :], z[0:HALF, :], ACT.Relu,
                                     bias=bias[0:HALF, layer:layer + 1]).then_inc(xk_ready[layer], 1)

            def feed0(g, t):
                act.wait_ge(l0_used, N0 * (g + 1))
                feed(0, g, t, z0[t % 2], slice(0, HALF))

            def feed1(g, t, n):
                act.wait_ge(plain_used, n + P_RING)
                feed(1, g, t, z1[t % 2], slice(HALF, P))

            def round0(g, t, k):
                act.wait_ge(sprod0_ready, S0 * g + k + 1)
                if not isinstance(g, int) or used0(g, k) > 0:
                    act.wait_ge(l0_used, used0(g, k))
                nc.scalar.activation(p0_hi[0:R0, buf0(t, k), :, :], sprod0[0:R0, :, :], ACT.Copy).then_inc(hi0_ready, 1)

            act.nop().then_inc(z2_read, 1)
            act.wait_ge(w_in, W_LOADS * 16)
            act.wait_ge(w0_ready, 2)
            for n in range(3):
                r = ROWS[n]
                nc.scalar.activation(w_hi[n][0:r, :, :], staged[n][0:r, :, :], ACT.Copy).then_inc(w_hi_ready, 1)
            for t in range(XT_HALVES):
                save_transposed(0, t)

            def round_high(units):
                for u in units:
                    if u.split:
                        act.wait_ge(sprod_ready, u.number + 1)
                        act.wait_ge(split_used, u.number + 1)
                        nc.scalar.activation(p_hi[:, u.buf, :, :], sprod[:, :, :], ACT.Copy).then_inc(hi_ready, 1)

            def splits_of(g, t, piece, last=False):
                return [u for u in units_of(g, t, piece, last) if u.split]

            def step(i, t, before, last):
                g = i * TILES + t
                final = last and t == TILES - 1
                more = not final
                splits = splits_of(g, t, 0)
                round_high(splits[:1])
                if more:
                    act.wait_ge(folds, folds_at(i - 1, (3, 5, 9)[t]) if t < TILES - 1 else folds_at(i, 1))
                    if t == 2 and before:
                        act.wait_ge(s_saved, i * 2 * 16)
                if before or t > 0:
                    if final:
                        act.wait_ge(folds, folds_at(i, 1))
                    direct2(g - 1, (t - 1) % TILES, done(L, g))
                round_high(splits[1:2])
                if more:
                    feed0(g + 1, (t + 1) % TILES)
                if not (last and t + 2 >= TILES):
                    round0(g + 2, t + 2, 1)
                if t == turn(i) and not last:
                    act.wait_ge(xT_saved, (i + 1) * XT_SAVES * 16)
                    act.wait_ge(pairs_saved, (i + 1) * PAIR_SAVES * 16)
                    save_transposed(i + 1, 0)
                round_high(splits[2:])
                if more:
                    splits = splits_of(g, t, 1)
                    round_high(splits[:2])
                    if not (last and t + 2 >= TILES):
                        round0(g + 2, t + 2, 2)
                    if t == turn(i) and not last:
                        save_transposed(i + 1, 1)
                    round_high(splits[2:])
                if not (last and t + 3 >= TILES):
                    round0(g + 3, t + 3, 0)
                splits = splits_of(g, t, 2, last)
                round_high(splits)
                if more:
                    feed1(g + 1, (t + 1) % TILES, done(L, g, 0, 1))

            def direct2(g, t, n):
                act.wait_ge(plain_used, n + P_RING)
                nc.scalar.activation(d2[:, t % 2, :], z2[:, :], ACT.Relu, bias=bias[:, 2:3]).then_inc(z2_read, 1)

            for k in range(S0):
                round0(0, 0, k)
            feed0(0, 0)
            splits = [u for u in first_units() if u.split]
            round_high(splits[:2])
            round0(1, 1, 0)
            round_high(splits[2:3])
            round0(1, 1, 1)
            round_high(splits[3:])
            round0(1, 1, 2)
            feed1(0, 0, count(L, 1))
            round0(2, 2, 0)
            for t in range(TILES):
                step(0, t, False, False)
            with act.Fori(1, BLOCKS - 1) as i:
                for t in range(TILES):
                    step(i, t, True, False)
            for t in range(TILES):
                step(BLOCKS - 1, t, True, True)
            act.wait_ge(mlp_in, MLP_LOADS * 16)
            for n, bank in enumerate((tp, z0[0], z0[1], z1[0])):
                act.wait_ge(dnT_ps, n + 1)
                nc.scalar.activation(dnT[:, n * COLS:(n + 1) * COLS], bank[0:NDENSE, :],
                                     ACT.Copy).then_inc(dnT_ready, 1)
            act.wait_ge(folds, folds_at(BLOCKS - 1, 3))
            direct2(LAST, TILES - 1, done(L, LAST, 0, 2))
            def first_layer(n):
                for m in range(H1 // P):
                    act.wait_ge(h1_ps, n * 4 + m + 1)
                    if n > 0:
                        act.wait_ge(h2_ps, n * 2)
                    nc.scalar.activation(h1[:, m, :], h1_bank[m][:, :], ACT.Relu,
                                         bias=bt1[:, m:m + 1]).then_inc(h1_ready, 1)

            groups = BATCH // COLS
            first_layer(0)
            for n in range(groups):
                for m in range(H2 // P):
                    act.wait_ge(h2_ps, n * 2 + m + 1)
                    if n > 0:
                        act.wait_ge(y_ps, n)
                    nc.scalar.activation(h2[:, m, :], h2_bank[m][:, :], ACT.Relu,
                                         bias=bt2[:, m:m + 1]).then_inc(h2_ready, 1)
                if n + 1 < groups:
                    first_layer(n + 1)
                act.wait_ge(y_ps, n + 1)
                if n == 0:
                    act.wait_ge(folds, folds_at(BLOCKS - 1, ADDS - 1))
                nc.scalar.activation(y_sb[:, n * COLS:(n + 1) * COLS], y_bank[0:1, :],
                                     ACT.Copy).then_inc(y_ready, 1)

        @block.vector
        def _(dve):
            dve.wait_ge(w_in, W_LOADS * 16)
            n = SPLIT_CHUNKS[0]
            for part, cs in ((staged[0], slice(0, n)), (w[0], slice(n, C0))):
                nc.vector.tensor_tensor(part[0:R0, :, :], part[0:R0, :, :], w0_swapped[0:R0, cs, :],
                                        ALU.add).then_inc(w0_ready, 1)
            for n in range(3):
                r = ROWS[n]
                dve.wait_ge(w_hi_ready, n + 1)
                nc.vector.tensor_tensor(w_lo[n][0:r, :, :], staged[n][0:r, :, :], w_hi[n][0:r, :, :],
                                        ALU.subtract).then_inc(w_lo_ready, 1)

            def multiply(u, b):
                xk = z0[b] if u.layer == 1 else z1[b]
                out, ready = (sprod, sprod_ready) if u.split else (prod[:, u.buf, :, :], plain_ready)
                c, n = u.chunk, u.full
                last = nc.vector.tensor_tensor(out[:, 0:n, :], xk[:, :].unsqueeze(1).to_broadcast([P, n, COLS]),
                                               xbc[:, b, c:c + n, :], ALU.mult)
                if u.half:
                    last = nc.vector.tensor_tensor(out[0:HALF, n, :], xk[0:HALF, :], xbc[0:HALF, b, c + n, :],
                                                   ALU.mult)
                last.then_inc(ready, 1)

            def subtract_high(u):
                dve.wait_ge(hi_ready, u.number + 1)
                dve.wait_ge(split_used, u.number + 1)
                nc.vector.tensor_tensor(p_lo[:, u.buf, :, :], sprod[:, :, :],
                                        p_hi[:, u.buf, :, :], ALU.subtract).then_inc(lo_ready, 1)

            def run(units, b, late=None):
                pending = None
                for u in units:
                    if late is not None and u.late:
                        dve.wait_ge(late_in[b], late)
                        late = None
                    if u.split:
                        dve.wait_ge(lo_ready, u.number + S_RING)
                    else:
                        dve.wait_ge(plain_used, u.number + 1)
                    multiply(u, b)
                    if pending is not None:
                        subtract_high(pending)
                    pending = u if u.split else None
                assert pending is None

            def run_layer1(units, g, b, loads):
                dve.wait_ge(early_in[b], loads * EARLY_LOADS * 16)
                dve.wait_ge(xk_ready[0], 2 * (g + 1))
                run(units, b, loads * LATE_LOADS * 16)

            def step(i, t, last):
                g = i * TILES + t
                dve.wait_ge(xk_ready[1], 2 * (g + 1))
                run(units_of(g, t, 0), t % 2)
                if not (last and t == TILES - 1):
                    run_layer1(units_of(g, t, 1), g + 1, (t + 1) % 2, i * (TILES // 2) + (t + 1) // 2 + 1)
                run(units_of(g, t, 2, last), t % 2)

            def first_layer0():
                def multiply0(out, k, ready):
                    _, c, n, _ = UNITS0[k]
                    nc.vector.tensor_tensor(out[0:R0, 0:n, :], x3[0:R0, :].unsqueeze(1).to_broadcast([R0, n, COLS]),
                                            xroll[0:R0, c:c + n, :], ALU.mult).then_inc(ready, 1)

                def subtract_high0(k):
                    dve.wait_ge(hi0_ready, k + 1)
                    if used0(0, k) > 0:
                        dve.wait_ge(l0_used, used0(0, k))
                    nc.vector.tensor_tensor(p0_lo[0:R0, buf0(0, k), :, :], sprod0[0:R0, :, :],
                                            p0_hi[0:R0, buf0(0, k), :, :], ALU.subtract).then_inc(lo0_ready, 1)

                dve.wait_ge(l0_in, L0_LOADS * 16)
                multiply0(sprod0, 0, sprod0_ready)
                multiply0(prod0, 3, prod0_ready)
                for k in range(S0):
                    subtract_high0(k)
                    if k + 1 < S0:
                        dve.wait_ge(lo0_ready, k + 1)
                        multiply0(sprod0, k + 1, sprod0_ready)

            first_layer0()
            dve.nop().then_inc(lo_ready, S_RING)
            run_layer1(first_units(), 0, 0, 1)
            with dve.Fori(0, BLOCKS - 1) as i:
                for t in range(TILES):
                    step(i, t, False)
            for t in range(TILES):
                step(BLOCKS - 1, t, True)

        @block.tensor
        def _(pe):
            def transpose_half(i, h):
                pe.wait_ge(gathered, (i + 1) * FIELDS * 16)
                if h > 0 or not isinstance(i, int):
                    pe.wait_ge(xT_ready, i * XT_HALVES + h)
                for d in range(4):
                    dims = slice(h * 4 + d, FIELDS * DIM, DIM // 2)
                    last = nc.tensor.transpose(tp[0:2 * FIELDS, d * P:(d + 1) * P],
                                               emb[:, :, :].rearrange("p f d -> p (f d)")[:, dims], ident[:, :])
                last.then_inc(transposed, 1)

            def split_chunk(out, w_hi, w_lo, hi, lo, start, stop):
                nc.tensor.matmul(out, w_hi, hi, start=start, stop=False)
                nc.tensor.matmul(out, w_hi, lo, start=False, stop=False)
                return nc.tensor.matmul(out, w_lo, hi, start=False, stop=stop)

            class Layer0:
                def __init__(self, g, t, spread):
                    self.g, self.t, self.spread, self.at = g, t, list(spread), 0
                    self.chunks = [(k, j) for k, unit in enumerate(UNITS0) for j in range(unit[2])]

                def behind(self, nth):
                    while self.at < len(self.spread) and self.spread[self.at] == nth:
                        contract0(self.g, self.t, *self.chunks[self.at])
                        self.at += 1

            def contract(units, z, nth, layer0, ends=False, begins=False):
                for m, u in enumerate(units):
                    if u.split:
                        pe.wait_ge(lo_ready, u.number + 1 + S_RING)
                    else:
                        pe.wait_ge(plain_ready, u.number + 1)
                    n = u.layer
                    for j in range(u.full + u.half):
                        ch = u.chunk + j
                        r = slice(0, HALF if j == u.full else P)
                        start = begins and m == 0 and j == 0
                        stop = ends and m == len(units) - 1 and j == u.full + u.half - 1
                        if u.split:
                            last = split_chunk(z[:, :], w_hi[n][r, ch, :], w_lo[n][r, ch, :], p_hi[r, u.buf, j, :],
                                               p_lo[r, u.buf, j, :], start, stop)
                        else:
                            last = nc.tensor.matmul(z[:, :], w[n][r, ch - SPLIT_CHUNKS[n], :], prod[r, u.buf, j, :],
                                                    start=start, stop=stop)
                    last.then_inc(split_used if u.split else plain_used, 1)
                    if not u.split:
                        if layer0 is not None:
                            layer0.behind(nth)
                        nth += 1

            def contract0(g, t, k, j):
                split, c, n, _ = UNITS0[k]
                z = z0[t % 2][:, :]
                if j == 0:
                    if split:
                        pe.wait_ge(lo0_ready, S0 * g + k + 1)
                    else:
                        pe.wait_ge(prod0_ready, g + 1)
                ch = c + j
                start, stop = k == 0 and j == 0, k == N0 - 1 and j == n - 1
                if split:
                    last = split_chunk(z, w_hi[0][0:R0, ch, :], w_lo[0][0:R0, ch, :], p0_hi[0:R0, buf0(t, k), j, :],
                                       p0_lo[0:R0, buf0(t, k), j, :], start, stop)
                else:
                    last = nc.tensor.matmul(z, w[0][0:R0, ch - SPLIT_CHUNKS[0], :], prod0[0:R0, j, :],
                                            start=start, stop=stop)
                if j == n - 1:
                    last.then_inc(l0_used, 1)

            def step(i, t, last):
                g = i * TILES + t
                transpose = t == turn(i) and not last
                layer0 = None if last and t + 2 >= TILES else Layer0(g + 2, t, SPREAD)
                if last and t == TILES - 1:
                    transpose_dense()
                if transpose:
                    transpose_half(i + 1, 0)
                pe.wait_ge(z2_read, g + 1)
                contract(units_of(g, t, 0), z2, 1, layer0, begins=True)
                nth = count(L, 0) + 1
                if transpose:
                    transpose_half(i + 1, 1)
                if not (last and t == TILES - 1):
                    contract(units_of(g, t, 1), z1[(t + 1) % 2], nth, layer0, begins=True, ends=True)
                    nth += count(L, 1)
                contract(units_of(g, t, 2, last), z2, nth, layer0, ends=True)

            def transpose_dense():
                pe.wait_ge(mlp_in, MLP_LOADS * 16)
                for n, bank in enumerate((tp, z0[0], z0[1], z1[0])):
                    for i in range(4):
                        last = nc.tensor.transpose(bank[0:NDENSE, i * P:(i + 1) * P], dn[:, n * 4 + i, :],
                                                   ident[:, :])
                    last.then_inc(dnT_ps, 1)

            pe.nop().then_inc(plain_used, P_RING)
            pe.nop().then_inc(split_used, S_RING)
            pe.wait_ge(ident_ok, 1)
            for h in range(XT_HALVES):
                transpose_half(0, h)
            pe.wait_ge(w_lo_ready, 3)
            Layer0(0, 0, [0] * C0).behind(0)
            contract(first_units(), z1[0], 1, Layer0(1, 1, SPREAD_FIRST), begins=True, ends=True)
            for t in range(TILES):
                step(0, t, False)
            with pe.Fori(1, BLOCKS - 1) as i:
                for t in range(TILES):
                    step(i, t, False)
            for t in range(TILES):
                step(BLOCKS - 1, t, True)

            def first_layer(n):
                cols = slice(n * COLS, (n + 1) * COLS)
                if n == BATCH // COLS - 1:
                    pe.wait_ge(folds, folds_at(BLOCKS - 1, ADDS - 1))
                for m in range(H1 // P):
                    if n > 0:
                        pe.wait_ge(h1_ready, (n - 1) * 4 + m + 1)
                    rows = slice(m * P, (m + 1) * P)
                    out = h1_bank[m][:, :]
                    nc.tensor.matmul(out, wt1[:, 0, rows], s01[:, cols], start=True, stop=False)
                    nc.tensor.matmul(out, wt1[:, 1, rows], s2[:, cols], start=False, stop=False)
                    nc.tensor.matmul(out, wt1d[:, rows], dnT[:, cols], start=False, stop=True).then_inc(h1_ps, 1)

            def second_layer(n):
                for m in range(H2 // P):
                    pe.wait_ge(h1_ready, (n + 1) * 4)
                    if n > 0:
                        pe.wait_ge(h2_ready, (n - 1) * 2 + m + 1)
                    elif m == 1:
                        pe.wait_ge(z2_read, BLOCKS * TILES + 1)
                    for k in range(H1 // P):
                        last = nc.tensor.matmul(h2_bank[m][:, :], wt2[:, k, m * P:(m + 1) * P], h1[:, k, :],
                                                start=(k == 0), stop=(k == H1 // P - 1))
                    last.then_inc(h2_ps, 1)

            def third_layer(n):
                pe.wait_ge(h2_ready, (n + 1) * 2)
                if n > 0:
                    pe.wait_ge(y_ready, n)
                for k in range(H2 // P):
                    last = nc.tensor.matmul(y_bank[0:1, :], wt3[:, k:k + 1], h2[:, k, :],
                                            start=(k == 0), stop=(k == H2 // P - 1))
                last.then_inc(y_ps, 1)

            pe.wait_ge(dnT_ready, 4)
            pe.wait_ge(s_in, 32)
            groups = BATCH // COLS
            first_layer(0)
            for n in range(groups):
                second_layer(n)
                if n + 1 < groups:
                    first_layer(n + 1)
                third_layer(n)


def kernel(**inputs):
    import numpy as np
    import concourse.bacc as bacc
    from concourse import mybir as mb
    from concourse.bass_utils import run_bass_kernel_spmd

    f32 = np.float32
    w0, w1, w2 = (np.asarray(inputs[f"L0_rec_w{n}"]) for n in range(3))
    fields, _, size = w0.shape
    u0 = 3
    c0 = (fields // 2 + 1 + u0 - 1) // u0
    w_cin0 = np.zeros((2, u0 * fields, c0, size), f32)
    for c in range(c0):
        for u in range(u0):
            r = u0 * c + u
            if r <= fields // 2:
                i = np.arange(fields)
                j = (i + r) % fields
                w_cin0[0, u * fields:(u + 1) * fields, c] = w0[i, j]
                if r > 0:
                    w_cin0[1, u * fields:(u + 1) * fields, c] = w0[j, i]

    def pairs(w):
        h, k, s = w.shape
        full = np.concatenate([w, w[h - h % 2:]])
        return np.ascontiguousarray(full.reshape(-1, 2, k, s).transpose(1, 2, 0, 3).reshape(2 * k, -1, s))

    a = {
        "ids": np.asarray(inputs["ids"]),
        "dense": np.asarray(inputs["dense_ctx"]),
        "w_cin0": w_cin0, "w_cin1": pairs(w1), "w_cin2": pairs(w2),
        "b_cin": np.stack([np.asarray(inputs[f"L0_rec_b{n}"]) for n in range(3)], axis=1),
        "w_top1": np.asarray(inputs["W_top1"]),
        "b_top1": np.asarray(inputs["b_top1"]).reshape(-1, 128).T,
        "w_top2": np.asarray(inputs["W_top2"]),
        "b_top2": np.asarray(inputs["b_top2"]).reshape(-1, 128).T,
        "w_top3": np.asarray(inputs["W_top3"]).reshape(-1, 128).T,
    }
    for f in range(fields):
        a[f"tbl_{f}"] = np.asarray(inputs[f"tbl_{f}"])
    a = {name: np.ascontiguousarray(v) for name, v in a.items()}

    nc = bacc.Bacc("TRN2", target_bir_lowering=False, num_devices=1)
    ap = {name: nc.dram_tensor(name, v.shape, mb.dt.from_np(v.dtype), kind="ExternalInput").ap()
          for name, v in a.items()}
    batch = a["ids"].shape[0]
    y = nc.dram_tensor("y", (batch, 1), mb.dt.float32, kind="ExternalOutput").ap()
    cin_tower(nc, ap["ids"], [ap[f"tbl_{f}"] for f in range(fields)], ap["dense"], ap["w_cin0"], ap["w_cin1"],
              ap["w_cin2"], ap["b_cin"], ap["w_top1"], ap["b_top1"], ap["w_top2"], ap["b_top2"], ap["w_top3"], y)
    r = run_bass_kernel_spmd(nc, [a], core_ids=[0])
    return r.results[0]["y"]
```
